# Optimizing a Trainium2 kernel written in Bass

```python
import numpy as np
import jax
import jax.numpy as jnp

def _softmax(x, axis=-1):
    return jax.nn.softmax(x, axis=axis)

def _gelu(x):
    return jax.nn.gelu(x, approximate=True)

def _silu(x):
    return jax.nn.silu(x)

def _sigmoid(x):
    return jax.nn.sigmoid(x)

def _layernorm(x, axis=-1, eps=1e-05):
    m = jnp.mean(x, axis=axis, keepdims=True)
    v = jnp.var(x, axis=axis, keepdims=True)
    return (x - m) / jnp.sqrt(v + eps)

def _scatter_add(tgt, idx, src, axis=0):
    return tgt.at[idx].add(src)

def _segment_sum(src, seg, n):
    return jax.ops.segment_sum(src, seg, n)
kernel_name = 'mk_cond_seq_d2_seqx_r8_d44fbd'

def setup_inputs(seed: int=0):
    np.random.seed(seed)
    _w = jnp.asarray

    def _rec_inputs():
        import jax
        import jax.numpy as jnp
        _rk = jax.random.key(seed)
        x = -0.0005207 + 1.001 * jax.random.normal(jax.random.fold_in(_rk, 1), (32, 128, 128), jnp.float32)
        _lenS = 128 - jax.random.randint(jax.random.fold_in(_rk, 7), (32,), 0, max(1, 128 // 4) + 1, jnp.int32)
        _lenS2 = 128 - jax.random.randint(jax.random.fold_in(_rk, 8), (32,), 0, max(1, 128 // 4) + 1, jnp.int32)
        itok_B_34_63 = jax.random.randint(jax.random.fold_in(_rk, 12), (32,), 34, 64, jnp.int32)
        fside_Bx16xSxS_0 = -1.47943e-05 + 1.00017 * jax.random.normal(jax.random.fold_in(_rk, 13), (32, 16, 128, 128), jnp.float32)
        itok_B_6_14 = jax.random.randint(jax.random.fold_in(_rk, 14), (32,), 6, 15, jnp.int32)
        _validS = jnp.arange(128)[None, :] < _lenS[:, None]
        _validS2 = jnp.arange(128)[None, :] < _lenS2[:, None]
        _causal = jnp.tril(jnp.ones((128, 128), dtype=bool))
        mask_Bx1xSxS_bk0 = jnp.logical_not(jnp.broadcast_to(_validS[:, None, None, :], (32, 1, 128, 128)))
        return (x, itok_B_34_63, fside_Bx16xSxS_0, itok_B_6_14, mask_Bx1xSxS_bk0)
    x, itok_B_34_63, fside_Bx16xSxS_0, itok_B_6_14, mask_Bx1xSxS_bk0 = _rec_inputs()

    def _L0_cond_setup():
        import jax, jax.numpy as jnp
        import numpy as np
        import math
        D_MODEL = 128
        N_HEAD = 16
        HEAD_DIM = D_MODEL // N_HEAD
        D_FF = 512
        NUM_STEPS = 100.0
        RESCALE = 4000.0
        EPS = 1e-05

        def _sin_emb(t):
            half = D_MODEL // 2
            x = t.astype(jnp.float32) / NUM_STEPS * RESCALE
            freqs = jnp.exp(jnp.arange(half, dtype=jnp.float32) * (-math.log(10000.0) / (half - 1)))
            e = x[:, None] * freqs[None, :]
            return jnp.concatenate([jnp.sin(e), jnp.cos(e)], axis=-1)

        def _ln(x):
            m = jnp.mean(x, axis=-1, keepdims=True)
            v = jnp.var(x, axis=-1, keepdims=True)
            return (x - m) / jnp.sqrt(v + EPS)

        def _gelu2(x):
            return x * jax.nn.sigmoid(1.702 * x)
        key = jax.random.key(seed)
        ks = jax.random.split(key, 24)
        B, S, D, F = (4, 64, D_MODEL, D_FF)
        std = 0.02
        inp = {'src': jax.random.normal(ks[0], (B, S, D), dtype=jnp.float32), 'src_mask': jax.random.randint(ks[1], (B, 1, S, S), 0, 2).astype(bool), 'timestep': jax.random.randint(ks[2], (B,), 0, 100, dtype=jnp.int32), 'attention_bias': jax.random.normal(ks[3], (B, N_HEAD, S, S), dtype=jnp.float32), 'W_ada': jax.random.normal(ks[4], (D, 2 * D), dtype=jnp.float32) * std, 'b_ada': jnp.zeros((2 * D,), dtype=jnp.float32), 'Wq': jax.random.normal(ks[5], (D, D), dtype=jnp.float32) * std, 'bq': jnp.zeros((D,), dtype=jnp.float32), 'Wk': jax.random.normal(ks[6], (D, D), dtype=jnp.float32) * std, 'bk': jnp.zeros((D,), dtype=jnp.float32), 'Wv': jax.random.normal(ks[7], (D, D), dtype=jnp.float32) * std, 'bv': jnp.zeros((D,), dtype=jnp.float32), 'Wo': jax.random.normal(ks[8], (D, D), dtype=jnp.float32) * std, 'bo': jnp.zeros((D,), dtype=jnp.float32), 'W1': jax.random.normal(ks[9], (D, F), dtype=jnp.float32) * std, 'b1': jnp.zeros((F,), dtype=jnp.float32), 'W2': jax.random.normal(ks[10], (F, D), dtype=jnp.float32) * std, 'b2': jnp.zeros((D,), dtype=jnp.float32), 'g2': jnp.ones((D,), dtype=jnp.float32), 'beta2': jnp.zeros((D,), dtype=jnp.float32)}
        return inp
    _L0_cond_all = _L0_cond_setup()
    _L0_cond_in = {k: v for k, v in _L0_cond_all.items() if k in ('W_ada', 'b_ada', 'Wq', 'bq', 'Wk', 'bk', 'Wv', 'bv', 'Wo', 'bo', 'W1', 'b1', 'W2', 'b2', 'g2', 'beta2')}
    del _L0_cond_all

    def _L1_cond_setup():
        import jax, jax.numpy as jnp
        import numpy as np
        D = 128
        E = 8
        FF = 512
        TOPK = 2
        S = 32
        SE = 64
        SH = 128
        B, T = (2, 256)

        def _forward(x, subject_ids, ln_g, ln_b, subj_emb, hyp_w1, hyp_b1, hyp_w2, hyp_b2, sty_w1, sty_b1, sty_w2, sty_b2, router_w, exp_w1, exp_b1, exp_w2, exp_b2):
            mu = x.mean(-1, keepdims=True)
            var = x.var(-1, keepdims=True)
            h = (x - mu) * jax.lax.rsqrt(var + 1e-05) * ln_g + ln_b
            m_t = h.mean(1, keepdims=True)
            v_t = h.var(1, keepdims=True)
            h_norm = (h - m_t) * jax.lax.rsqrt(v_t + 1e-08)
            se = subj_emb[subject_ids]
            hyp = jax.nn.relu(se @ hyp_w1 + hyp_b1) @ hyp_w2 + hyp_b2
            sty = jax.nn.relu(hyp @ sty_w1 + sty_b1) @ sty_w2 + sty_b2
            gamma, beta = jnp.split(sty, 2, axis=-1)
            gamma = jax.nn.softplus(gamma) + 1e-08
            h = h_norm * gamma[:, None, :] + beta[:, None, :]
            h_flat = h.reshape(-1, D)
            probs = jax.nn.softmax(h_flat @ router_w, axis=-1)
            gates, idx = jax.lax.top_k(probs, TOPK)
            gates = gates / gates.sum(-1, keepdims=True)
            N = h_flat.shape[0]
            combine = jnp.zeros((N, E), h_flat.dtype).at[jnp.arange(N)[:, None], idx].add(gates)
            hid = jax.nn.relu(jnp.einsum('nd,edf->nef', h_flat, exp_w1) + exp_b1)
            eout = jnp.einsum('nef,efd->ned', hid, exp_w2) + exp_b2
            y = jnp.einsum('ned,ne->nd', eout, combine)
            return x + y.reshape(x.shape)
        key = jax.random.key(seed)
        ks = jax.random.split(key, 16)
        n = lambda k, sh, s=0.02: jax.random.normal(k, sh, dtype=jnp.float32) * s
        return {'x': jax.random.normal(ks[0], (B, T, D), dtype=jnp.float32), 'subject_ids': jax.random.randint(ks[1], (B,), 0, S), 'ln_g': jnp.ones((D,), jnp.float32), 'ln_b': jnp.zeros((D,), jnp.float32), 'subj_emb': n(ks[2], (S, SE)), 'hyp_w1': n(ks[3], (SE, SH), 1.0 / np.sqrt(SE)), 'hyp_b1': jnp.zeros((SH,), jnp.float32), 'hyp_w2': n(ks[4], (SH, SH), 1.0 / np.sqrt(SH)), 'hyp_b2': jnp.zeros((SH,), jnp.float32), 'sty_w1': n(ks[5], (SH, SH // 2), 1.0 / np.sqrt(SH)), 'sty_b1': jnp.zeros((SH // 2,), jnp.float32), 'sty_w2': n(ks[6], (SH // 2, 2 * D), 1.0 / np.sqrt(SH // 2)), 'sty_b2': jnp.zeros((2 * D,), jnp.float32), 'router_w': n(ks[7], (D, E), 1.0 / np.sqrt(D)), 'exp_w1': n(ks[8], (E, D, FF), 1.0 / np.sqrt(D)), 'exp_b1': jnp.zeros((E, FF), jnp.float32), 'exp_w2': n(ks[9], (E, FF, D), 1.0 / np.sqrt(FF)), 'exp_b2': jnp.zeros((E, D), jnp.float32)}
    _L1_cond_all = _L1_cond_setup()
    _L1_cond_in = {k: v for k, v in _L1_cond_all.items() if k in ('ln_g', 'ln_b', 'subj_emb', 'hyp_w1', 'hyp_b1', 'hyp_w2', 'hyp_b2', 'sty_w1', 'sty_b1', 'sty_w2', 'sty_b2', 'router_w', 'exp_w1', 'exp_b1', 'exp_w2', 'exp_b2')}
    del _L1_cond_all
    return {'x': x, 'itok_B_34_63': itok_B_34_63, 'fside_Bx16xSxS_0': fside_Bx16xSxS_0, 'itok_B_6_14': itok_B_6_14, 'mask_Bx1xSxS_bk0': mask_Bx1xSxS_bk0, 'L0_cond_W_ada': _L0_cond_in['W_ada'], 'L0_cond_b_ada': _L0_cond_in['b_ada'], 'L0_cond_Wq': _L0_cond_in['Wq'], 'L0_cond_bq': _L0_cond_in['bq'], 'L0_cond_Wk': _L0_cond_in['Wk'], 'L0_cond_bk': _L0_cond_in['bk'], 'L0_cond_Wv': _L0_cond_in['Wv'], 'L0_cond_bv': _L0_cond_in['bv'], 'L0_cond_Wo': _L0_cond_in['Wo'], 'L0_cond_bo': _L0_cond_in['bo'], 'L0_cond_W1': _L0_cond_in['W1'], 'L0_cond_b1': _L0_cond_in['b1'], 'L0_cond_W2': _L0_cond_in['W2'], 'L0_cond_b2': _L0_cond_in['b2'], 'L0_cond_g2': _L0_cond_in['g2'], 'L0_cond_beta2': _L0_cond_in['beta2'], 'L1_cond_ln_g': _L1_cond_in['ln_g'], 'L1_cond_ln_b': _L1_cond_in['ln_b'], 'L1_cond_subj_emb': _L1_cond_in['subj_emb'], 'L1_cond_hyp_w1': _L1_cond_in['hyp_w1'], 'L1_cond_hyp_b1': _L1_cond_in['hyp_b1'], 'L1_cond_hyp_w2': _L1_cond_in['hyp_w2'], 'L1_cond_hyp_b2': _L1_cond_in['hyp_b2'], 'L1_cond_sty_w1': _L1_cond_in['sty_w1'], 'L1_cond_sty_b1': _L1_cond_in['sty_b1'], 'L1_cond_sty_w2': _L1_cond_in['sty_w2'], 'L1_cond_sty_b2': _L1_cond_in['sty_b2'], 'L1_cond_router_w': _L1_cond_in['router_w'], 'L1_cond_exp_w1': _L1_cond_in['exp_w1'], 'L1_cond_exp_b1': _L1_cond_in['exp_b1'], 'L1_cond_exp_w2': _L1_cond_in['exp_w2'], 'L1_cond_exp_b2': _L1_cond_in['exp_b2']}

def reference(x, itok_B_34_63, fside_Bx16xSxS_0, itok_B_6_14, mask_Bx1xSxS_bk0, L0_cond_W_ada, L0_cond_b_ada, L0_cond_Wq, L0_cond_bq, L0_cond_Wk, L0_cond_bk, L0_cond_Wv, L0_cond_bv, L0_cond_Wo, L0_cond_bo, L0_cond_W1, L0_cond_b1, L0_cond_W2, L0_cond_b2, L0_cond_g2, L0_cond_beta2, L1_cond_ln_g, L1_cond_ln_b, L1_cond_subj_emb, L1_cond_hyp_w1, L1_cond_hyp_b1, L1_cond_hyp_w2, L1_cond_hyp_b2, L1_cond_sty_w1, L1_cond_sty_b1, L1_cond_sty_w2, L1_cond_sty_b2, L1_cond_router_w, L1_cond_exp_w1, L1_cond_exp_b1, L1_cond_exp_w2, L1_cond_exp_b2):
    import jax
    import jax.numpy as jnp

    def _L0_cond_ref(src, src_mask, timestep, attention_bias, W_ada, b_ada, Wq, bq, Wk, bk, Wv, bv, Wo, bo, W1, b1, W2, b2, g2, beta2):
        import jax, jax.numpy as jnp
        import numpy as np
        import math
        D_MODEL = 128
        N_HEAD = 16
        HEAD_DIM = D_MODEL // N_HEAD
        D_FF = 512
        NUM_STEPS = 100.0
        RESCALE = 4000.0
        EPS = 1e-05

        def _sin_emb(t):
            half = D_MODEL // 2
            x = t.astype(jnp.float32) / NUM_STEPS * RESCALE
            freqs = jnp.exp(jnp.arange(half, dtype=jnp.float32) * (-math.log(10000.0) / (half - 1)))
            e = x[:, None] * freqs[None, :]
            return jnp.concatenate([jnp.sin(e), jnp.cos(e)], axis=-1)

        def _ln(x):
            m = jnp.mean(x, axis=-1, keepdims=True)
            v = jnp.var(x, axis=-1, keepdims=True)
            return (x - m) / jnp.sqrt(v + EPS)

        def _gelu2(x):
            return x * jax.nn.sigmoid(1.702 * x)
        B, S, D = src.shape
        emb = jax.nn.silu(_sin_emb(timestep)) @ W_ada + b_ada
        scale, shift = jnp.split(emb[:, None, :], 2, axis=-1)
        x = _ln(src) * (1.0 + scale) + shift
        q = (x @ Wq + bq).reshape(B, S, N_HEAD, HEAD_DIM).transpose(0, 2, 1, 3)
        k = (x @ Wk + bk).reshape(B, S, N_HEAD, HEAD_DIM).transpose(0, 2, 1, 3)
        v = (x @ Wv + bv).reshape(B, S, N_HEAD, HEAD_DIM).transpose(0, 2, 1, 3)
        scores = jnp.einsum('bhqd,bhkd->bhqk', q / math.sqrt(HEAD_DIM), k)
        scores = scores + attention_bias
        scores = jnp.where(src_mask, -jnp.inf, scores.astype(jnp.float32))
        probs = jax.nn.softmax(scores, axis=-1).astype(v.dtype)
        ctx = jnp.einsum('bhqk,bhkd->bhqd', probs, v)
        ctx = ctx.transpose(0, 2, 1, 3).reshape(B, S, D)
        x = x + (ctx @ Wo + bo)
        h = _ln(x) * g2 + beta2
        ff = _gelu2(h @ W1 + b1) @ W2 + b2
        return x + ff

    def _L1_cond_ref(x, subject_ids, ln_g, ln_b, subj_emb, hyp_w1, hyp_b1, hyp_w2, hyp_b2, sty_w1, sty_b1, sty_w2, sty_b2, router_w, exp_w1, exp_b1, exp_w2, exp_b2):
        import jax, jax.numpy as jnp
        import numpy as np
        D = 128
        E = 8
        FF = 512
        TOPK = 2
        S = 32
        SE = 64
        SH = 128
        B, T = (2, 256)

        def _forward(x, subject_ids, ln_g, ln_b, subj_emb, hyp_w1, hyp_b1, hyp_w2, hyp_b2, sty_w1, sty_b1, sty_w2, sty_b2, router_w, exp_w1, exp_b1, exp_w2, exp_b2):
            mu = x.mean(-1, keepdims=True)
            var = x.var(-1, keepdims=True)
            h = (x - mu) * jax.lax.rsqrt(var + 1e-05) * ln_g + ln_b
            m_t = h.mean(1, keepdims=True)
            v_t = h.var(1, keepdims=True)
            h_norm = (h - m_t) * jax.lax.rsqrt(v_t + 1e-08)
            se = subj_emb[subject_ids]
            hyp = jax.nn.relu(se @ hyp_w1 + hyp_b1) @ hyp_w2 + hyp_b2
            sty = jax.nn.relu(hyp @ sty_w1 + sty_b1) @ sty_w2 + sty_b2
            gamma, beta = jnp.split(sty, 2, axis=-1)
            gamma = jax.nn.softplus(gamma) + 1e-08
            h = h_norm * gamma[:, None, :] + beta[:, None, :]
            h_flat = h.reshape(-1, D)
            probs = jax.nn.softmax(h_flat @ router_w, axis=-1)
            gates, idx = jax.lax.top_k(probs, TOPK)
            gates = gates / gates.sum(-1, keepdims=True)
            N = h_flat.shape[0]
            combine = jnp.zeros((N, E), h_flat.dtype).at[jnp.arange(N)[:, None], idx].add(gates)
            hid = jax.nn.relu(jnp.einsum('nd,edf->nef', h_flat, exp_w1) + exp_b1)
            eout = jnp.einsum('nef,efd->ned', hid, exp_w2) + exp_b2
            y = jnp.einsum('ned,ne->nd', eout, combine)
            return x + y.reshape(x.shape)
        return _forward(x, subject_ids, ln_g, ln_b, subj_emb, hyp_w1, hyp_b1, hyp_w2, hyp_b2, sty_w1, sty_b1, sty_w2, sty_b2, router_w, exp_w1, exp_b1, exp_w2, exp_b2)
    x = _L0_cond_ref(x, mask_Bx1xSxS_bk0, itok_B_34_63, fside_Bx16xSxS_0, L0_cond_W_ada, L0_cond_b_ada, L0_cond_Wq, L0_cond_bq, L0_cond_Wk, L0_cond_bk, L0_cond_Wv, L0_cond_bv, L0_cond_Wo, L0_cond_bo, L0_cond_W1, L0_cond_b1, L0_cond_W2, L0_cond_b2, L0_cond_g2, L0_cond_beta2)
    x = _L1_cond_ref(x, itok_B_6_14, L1_cond_ln_g, L1_cond_ln_b, L1_cond_subj_emb, L1_cond_hyp_w1, L1_cond_hyp_b1, L1_cond_hyp_w2, L1_cond_hyp_b2, L1_cond_sty_w1, L1_cond_sty_b1, L1_cond_sty_w2, L1_cond_sty_b2, L1_cond_router_w, L1_cond_exp_w1, L1_cond_exp_b1, L1_cond_exp_w2, L1_cond_exp_b2)
    return x

_drawn_inputs = setup_inputs


def setup_inputs(seed=0):
    import zlib

    import numpy as np

    out = dict(_drawn_inputs(seed))
    spreads = {'L0_cond_b_ada': (0.0, 0.1),
     'L0_cond_bq': (0.0, 0.8),
     'L0_cond_bk': (0.0, 0.8),
     'L0_cond_bv': (0.0, 0.36),
     'L0_cond_bo': (0.0, 0.1),
     'L0_cond_b1': (0.0, 0.1),
     'L0_cond_b2': (0.0, 0.1),
     'L0_cond_g2': (1.0, 0.2),
     'L0_cond_beta2': (0.0, 0.584),
     'L1_cond_ln_g': (1.0, 0.6),
     'L1_cond_ln_b': (0.0, 0.8),
     'L1_cond_hyp_b1': (0.0, 0.1),
     'L1_cond_hyp_b2': (0.0, 0.1),
     'L1_cond_sty_b1': (0.0, 0.1),
     'L1_cond_sty_b2': (0.0, 0.1),
     'L1_cond_exp_b1': (0.0, 0.1),
     'L1_cond_exp_b2': (0.0, 0.1)}
    factors = {'fside_Bx16xSxS_0': 2.724, 'L0_cond_Wq': 7.717, 'L0_cond_Wk': 8.0}
    for name, (base, spread) in spreads.items():
        noise = np.random.default_rng([zlib.crc32(name.encode()), seed]).standard_normal(out[name].shape)
        drawn = base * np.exp(spread * noise) if base else spread * noise
        out[name] = jnp.asarray(drawn.astype(out[name].dtype))
    for name, factor in factors.items():
        out[name] = (out[name] * factor).astype(out[name].dtype)
    return out
```

```python
from contextlib import ExitStack

import numpy as np

import concourse.bass as bass
from concourse import mybir

ALU = mybir.AluOpType
ACT = mybir.ActivationFunctionType
AX = mybir.AxisListType
F32 = mybir.dt.float32
BF16 = mybir.dt.bfloat16
I32 = mybir.dt.int32
U32 = mybir.dt.uint32
U8 = mybir.dt.uint8

P = 128
NB = 32
H, HD = 16, 8
FF = 512
NCH = FF // P
E = 8
TOPK = 2
SLOTS = 8
Q_PART = [0, 0, 0, 1, 1, 1, 2, 2]
K_PART = [0, 1, 2, 0, 1, 2, 0, 1]
BK = 64 + NCH
VC = HD + 1
VW = 8 * VC
MASKED = -3.0e38
W_WIDTH = [2 * P, P, P, P, P, P, 64, 8]
W_AT = [sum(W_WIDTH[:k]) for k in range(len(W_WIDTH))]
W_COLS = sum(W_WIDTH)
ROW = 138
DEST, GATE = 136, 137
TOKENS = NB * P
REGION = TOKENS + P
MAX_TILES = TOPK * TOKENS // P + E - 1
TILES = -(-MAX_TILES // 4) * 4
NOWHERE = 4 * TOPK * TOKENS
EPS, EPS_T = 1e-5, 1e-8


X_W1, X_W2, X_B1, X_B2, EXPERT = 0, FF, 2 * FF, 2 * FF + NCH, 2 * FF + NCH + P
(C_BADA_S, C_BADA_H, C_BQ, C_BK, C_G2, C_BETA2, C_LNG, C_LNB, C_HB1, C_HB2, C_SB1, C_SB2G, C_SB2B, C_FREQ,
 C_PHASE) = range(15)
N_COLS = 15


class At:

    def __init__(self, unit, i, c, count=None):
        self.unit, self.i, self.c = unit, i, c
        self.count = count or (NB if unit == 4 else NB // 2)

    @property
    def v(self):
        return self.i * self.unit + self.c

    def ring(self, r):
        return self.c % r

    def turn(self, r):
        return self.i * (self.unit // r) + self.c // r

    def __bool__(self):
        return not isinstance(self.i, int) or 0 <= self.v < self.count


class Slot:

    def __init__(self, i, b):
        self.i, self.b, self.odd = i, b, b % 2 == 1

    def tile(self, lag):
        return At(4, self.i, self.b - lag, TILES)

    def batch(self, lag):
        return At(4, self.i, self.b - lag)

    def pair(self, ahead):
        return At(2, self.i, (self.b + ahead) // 2)


def wait(eng, sem, value):
    if not isinstance(value, int) or value > 0:
        eng.wait_ge(sem, value)


def wait_first(eng, *options):
    for exists, sem, value in options:
        if exists:
            wait(eng, sem, value)
            return


def settle(eng, n):
    if not isinstance(n.i, int):
        eng.nop(nofuse=True)


FIRST_SLOT, LOOP_FROM, LOOP_TO, LAST_SLOT = -4, 2, 6, 38


def all_slots(eng, slot, after=None):
    for s in range(FIRST_SLOT, 4 * LOOP_FROM):
        slot(Slot(s // 4, s % 4))
        if after and s in after:
            after[s]()
    with eng.Fori(LOOP_FROM, LOOP_TO) as i:
        for b in range(4):
            slot(Slot(i, b))
    for s in range(4 * LOOP_TO, LAST_SLOT + 1):
        slot(Slot(s // 4, s % 4))


def all_tiles(eng, slot):
    for s in range(0, 8):
        slot(Slot(s // 4, s % 4))
    with eng.Fori(2, TILES // 4) as i:
        for b in range(4):
            slot(Slot(i, b))
    for s in range(TILES, TILES + 4):
        slot(Slot(s // 4, s % 4))


def build(nc, a, out, phases=3):
    ctx = ExitStack()
    with ctx:
        def sb(name, shape, dt=F32):
            return ctx.enter_context(nc.sbuf_tensor(name, shape, dt))

        def sem(name):
            return ctx.enter_context(nc.semaphore(name))

        part_scr = nc.dram_tensor("part_scr", (2, 6, P, 2 * P), BF16, kind="Internal").ap()
        rows_scr = nc.dram_tensor("rows_scr", (E * REGION, ROW), F32, kind="Internal").ap()
        y_scr = nc.dram_tensor("y_scr", (TOPK * TOKENS + P, P), F32, kind="Internal").ap()

        ident = sb("ident", [P, P])
        ident_b = sb("ident_b", [P, P], BF16)
        before = sb("before", [P, P], BF16)
        ones_b = sb("ones_b", [P, P], BF16)
        m_half = sb("m_half", [P, 4])
        iota_e = sb("iota_e", [P, E])
        iota_p = sb("iota_p", [P, 1])
        dest_tab = sb("dest_tab", [P, NB, TOPK])
        w_sq = sb("w_sq", [P, W_COLS])
        w_ada, w_q, w_k, w_v, w_o, hyp_w2, sty_w1, w_r = (
            w_sq[:, at:at + n] for at, n in zip(W_AT, W_WIDTH))
        w_1 = sb("w_1", [P, FF])
        w_2 = sb("w_2", [P, NCH, P])
        cols = sb("cols", [P, N_COLS])
        b1_f = sb("b1_f", [BK, P])
        b1_r = sb("b1_r", [BK, 2, P])
        b1_t = sb("b1_t", [BK, 3, P], BF16)
        b1_p = sb("b1_p", [BK, P], BF16)
        sel = sb("sel", [BK, NCH, P], BF16)
        rows_bc = sb("rows_bc", [P, 3, P])
        bv_bc, bo_bc, b2_bc = (rows_bc[:, k] for k in range(3))
        ints = sb("ints", [P, 2, NB], I32)
        subj = sb("subj", [NB, 64])
        w_64 = sb("w_64", [64, 3 * P])
        hyp_w1, sty_w2 = w_64[:, 0:P], w_64[:, P:3 * P]
        pre = sb("pre", [P, 12, NB])
        scale1 = sb("scale1", [P, NB])
        shift = sb("shift", [P, NB])
        gamma = sb("gamma", [P, NB, 2])
        beta = sb("beta", [P, NB])
        w_e = sb("w_e", [P, E, EXPERT])
        resid = sb("resid", [P, NB, P])

        zero_row = sb("zero_row", [P, ROW])
        pad_f = sb("pad_f", [P, E])
        pad_i = sb("pad_i", [P, E], I32)
        base_e = sb("base_e", [P, E])
        run = sb("run", [P, 4, 4 + E])
        past = sb("past", [P, 3, E])
        tc = sb("tc", [P, 4])
        tab = sb("tab", [1, 2, P], I32)
        rows_in = sb("rows_in", [P, 4, ROW])
        dest_i = sb("dest_i", [P, 4], I32)
        gate_m = sb("gate_m", [P, 4])
        h_mt = sb("h_mt", [P, 2, P])
        hid = sb("hid", [P, 2, NCH, P])
        y_b = sb("y_b", [P, 2, P])
        y_g = sb("y_g", [P, 4, P])
        x_in = sb("x_in", [P, 2, 2, P])
        mask_u8 = sb("mask_u8", [P, 2, 2, P], U8)
        mask_b = sb("mask_b", [P, 2, 2, P], BF16)
        x_n = sb("x_n", [P, 2, P])
        x_t = sb("x_t", [P, 2, 2 * P])
        qk_f = sb("qk_f", [P, 2 * 2 * P])
        qk_r = sb("qk_r", [P, 2 * 2 * P])
        qk_p = sb("qk_p", [P, 3, 2, 2 * P], BF16)
        q_st = sb("q_st", [P, 2, 8, 2 * P], BF16)
        k_st = sb("k_st", [P, 2, 2, 8, 2 * P], BF16)
        v_pad = sb("v_pad", [P, 4, 2, 8, VW])
        score = sb("score", [P, 4, H, P])
        top = sb("top", [P, 2, H])
        prob = sb("prob", [P, 2, 4 * P])
        ctx_u = sb("ctx_u", [VW, 2 * P])
        r_den = sb("r_den", [P, H])
        ctx_n = sb("ctx_n", [P, P])
        ctx_t = sb("ctx_t", [P, P])
        x_2b = sb("x_2b", [P, P])
        n_2 = sb("n_2", [P, P])
        h_2 = sb("h_2", [P, P])
        up_t = sb("up_t", [P, NCH, P])
        act_1 = sb("act_1", [P, NCH, P])
        z_3 = sb("z_3", [P, P])
        h_t = sb("h_t", [P, 2, P])
        h_f = sb("h_f", [P, P])
        row = sb("row", [P, 2, TOPK, ROW])
        stat_f = sb("stat_f", [P, 2, 6])
        stat_2, stat_3, stat_t = (sb(n, [P, 6]) for n in ("stat_2", "stat_3", "stat_t"))
        mv_f = sb("mv_f", [P, 2, 2, 2])
        mv_2, mv_3, mv_t = (sb(n, [P, 2, 2]) for n in ("mv_2", "mv_3", "mv_t"))
        rs_f = sb("rs_f", [P, 2, 2])
        rs_2, rs_3, rs_t = (sb(n, [P, 2]) for n in ("rs_2", "rs_3", "rs_t"))
        coef = sb("coef", [P, 3])
        top8 = sb("top8", [P, 8])
        ix8 = sb("ix8", [P, 8], U32)
        ix_f = sb("ix_f", [P, TOPK])
        gate = sb("gate", [P, 4])
        hot = sb("hot", [P, 2, TOPK, E])
        hot_b = sb("hot_b", [P, E], BF16)
        count = sb("count", [P, E])
        pos = sb("pos", [P, E])
        pick = sb("pick", [P, TOPK, E])
        slot_f = sb("slot_f", [P, TOPK])
        slot_i = sb("slot_i", [P, 2, TOPK], I32)

        def res(n):
            return resid[:, bass.ds(n.v, 1), :].rearrange("p o d -> p (o d)")

        def bank(name):
            return ctx.enter_context(nc.psum_tensor(name, [P, 512], F32))

        s_ps = [bank("s_ps0"), bank("s_ps1")]
        t_ps = [bank("t_ps0"), bank("t_ps1")]
        c_ps = bank("c_ps")
        m0, m1, m2 = bank("m0"), bank("m1"), bank("m2")

        w_loaded, c_loaded, e_loaded = sem("w_loaded"), sem("c_loaded"), sem("e_loaded")
        const_ready = sem("const_ready")
        dve_const = sem("dve_const")
        pre_dve, pre_act, pre_pe, style_dve = sem("pre_dve"), sem("pre_act"), sem("pre_pe"), sem("style_dve")
        x_loaded = [sem(f"x_loaded{r}") for r in range(2)]
        mask_loaded = [sem(f"mask_loaded{r}") for r in range(2)]
        bias_loaded = [sem(f"bias_loaded{r}") for r in range(4)]
        parts_stored = sem("parts_stored")
        stack_loaded = [sem(f"stack_loaded{r}") for r in range(2)]
        (p_xt, p_xb, p_qk, p_v, p_s, p_t, p_pv, p_den, p_ct, p_wo, p_n2, p_up, p_dn, p_zt, p_rr, p_pos) = (
            sem(n) for n in ("p_xt", "p_xb", "p_qk", "p_v", "p_s", "p_t", "p_pv", "p_den", "p_ct", "p_wo", "p_n2",
                             "p_up", "p_dn", "p_zt", "p_rr", "p_pos"))
        (a_xt, a_qk, a_exp, a_c, a_ct, a_h2, a_tanh, a_ht, a_rr, a_gate, a_hf, a_mask,
         a_part) = (
            sem(n) for n in ("a_xt", "a_qk", "a_exp", "a_c", "a_ct", "a_h2", "a_tanh", "a_ht", "a_rr", "a_gate", "a_hf",
                             "a_mask", "a_part"))
        (v_statf, v_xn, v_xb, v_v, v_part, v_s, v_ctx, v_x2, v_n2, v_u, v_gelu, v_x3, v_z, v_statt,
         v_hf, v_route, v_pos) = (
            sem(n) for n in ("v_statf", "v_xn", "v_xb", "v_v", "v_part", "v_s", "v_ctx", "v_x2", "v_n2",
                             "v_u", "v_gelu", "v_x3", "v_z", "v_statt", "v_hf", "v_route", "v_pos"))
        v_gates = sem("v_gates")
        v_mv, v_posc, v_hf3, v_rt = sem("v_mv"), sem("v_posc"), sem("v_hf3"), sem("v_rt")
        (g_rf, g_r2, g_r3, g_rt, g_sub, g_b2) = (sem(n) for n in ("g_rf", "g_r2", "g_r3", "g_rt", "g_sub", "g_b2"))
        g_rows = [sem(f"g_rows{r}") for r in range(2)]

        z_rows, z_rows_sp, z_rows_act, t_tab, mp_tab = sem("z_rows"), sem("z_rows_sp"), sem("z_rows_act"), sem("t_tab"), sem("mp_tab")
        b1_ready = sem("b1_ready")
        B1_STEPS = 14
        CONSTS = 27
        PADS_POOL, PADS_SP = 1, 4
        TAB_STEPS = 15
        rows_loaded = [sem(f"rows_loaded{r}") for r in range(4)]
        (mp_t, mp_up, mp_dn, ma_ht, ma_relu, ma_y, mv_meta, mv_w, mv_y) = (
            sem(n) for n in ("mp_t", "mp_up", "mp_dn", "ma_ht", "ma_relu", "ma_y", "mv_meta", "mv_w", "mv_y"))
        y_out = [sem(f"y_out{r}") for r in range(4)]
        y_loaded = [sem(f"y_loaded{r}") for r in range(4)]
        summed, stored = sem("summed"), sem("stored")

        N_C, N_E, N_W = 3, 3 + E, 8
        PART = P * 2 * P

        w_now = [score[:, r].rearrange("p h t -> p (h t)")[:, 0:EXPERT] for r in range(4)]

        block = ctx.enter_context(nc.Block())

        @block.sync
        def _(sp):
            def load(dst, src, sem_):
                sp.dma_start(dst, src).then_inc(sem_, 16)

            load(ints[:], a["ints"].rearrange("(o k) b -> o k b", o=1).broadcast_to((P, 2, NB)), c_loaded)
            load(cols[:], a["cols"], c_loaded)
            load(x_in[:, 0], a["x"][0:2].rearrange("b t d -> t b d"), x_loaded[0])
            load(w_sq[:], a["w_sq"], c_loaded)
            load(x_in[:, 1], a["x"][2:4].rearrange("b t d -> t b d"), x_loaded[1])
            load(rows_bc[:], a["rows"].rearrange("(o k) d -> o k d", o=1).broadcast_to((P, 3, P)), w_loaded)
            load(subj[:], a["subj_emb"], w_loaded)
            load(w_64[:], a["w_64"], w_loaded)
            load(w_1[:], a["w1"], w_loaded)
            load(w_2[:], a["w2"].rearrange("(c p) n -> p c n", p=P), w_loaded)
            for k in range(3):
                load(b1_f[32 * k:32 * k + NCH], a["b1"], w_loaded)

            def load_x(j):
                wait(sp, v_xn, 2 * (j.v - 1))
                settle(sp, j)
                sp.dma_start(x_in[:, j.ring(2)], a["x"][bass.ds(j.v * 2, 2)].rearrange("b t d -> t b d")).then_inc(
                    x_loaded[j.ring(2)], 16)

            def load_mask(j):
                wait(sp, a_mask, j.v - 1)
                settle(sp, j)
                sp.dma_start(mask_u8[:, j.ring(2)], a["mask"][bass.ds(j.v * 2, 2)].rearrange("b q k -> q b k")).then_inc(
                    mask_loaded[j.ring(2)], 16)

            def load_bias(n):
                wait(sp, p_t, 4 * (n.v - 3))
                settle(sp, n)
                for h0 in (0, 8):
                    sp.dma_start(score[:, n.ring(4), h0:h0 + 8],
                                 a["bias"][bass.ds(n.v, 1), h0:h0 + 8].rearrange("o h q k -> q (o h) k")).then_inc(
                        bias_loaded[n.ring(4)], 16)

            def store_parts(j):
                if not isinstance(j.v, int) or j.v >= 2:
                    sp.wait_ge(stack_loaded[j.ring(2)], 16 * 12 * (j.turn(2)))
                settle(sp, j)
                sp.wait_ge(v_part, 4 * (j.v + 1))
                settle(sp, j)
                for half in range(2):
                    sp.dma_start(part_scr[j.ring(2), 3 * half:3 * half + 3].rearrange("a p t -> p a t"),
                                 qk_p[:, :, half, :]).then_inc(parts_stored, 16)

            def load_stack(j):
                r = j.ring(2)
                sp.wait_ge(parts_stored, 32 * (j.v + 1))
                settle(sp, j)
                wait(sp, p_s, 8 * (j.v - 1))
                settle(sp, j)
                base = r * 6 * PART
                for hh in range(2):
                    for s0, n_sl in ((0, 3), (3, 3), (6, 2)):
                        rows = slice(64 * hh + HD * s0, 64 * hh + HD * (s0 + n_sl))
                        q_src = bass.AP(tensor=part_scr.tensor, offset=base + Q_PART[s0] * PART + hh * 64 * 2 * P,
                                        ap=[[0, n_sl], [8 * 2 * P, HD], [1, 8 * 2 * P]])
                        k_src = bass.AP(tensor=part_scr.tensor, offset=base + 3 * PART + hh * 64 * 2 * P,
                                        ap=[[PART, n_sl], [8 * 2 * P, HD], [1, 8 * 2 * P]])
                        sp.dma_start(q_st[rows, r].rearrange("p a t -> p (a t)"), q_src).then_inc(stack_loaded[r], 16)
                        sp.dma_start(k_st[rows, r, hh].rearrange("p a t -> p (a t)"), k_src).then_inc(stack_loaded[r], 16)

            load_mask(At(2, 0, 0))
            load_bias(At(4, 0, 0))
            load_bias(At(4, 0, 1))

            def load_experts():
                sp.dma_start(w_e[:, :, X_W1:X_W2], a["exp_w1"].rearrange("e p n -> p e n")).then_inc(e_loaded, 16)
                for e in range(E):
                    sp.dma_start(w_e[:, e, X_W2:X_B1].rearrange("p (c n) -> p c n", c=NCH),
                                 a["exp_w2"][e].rearrange("(c p) n -> p c n", p=P)).then_inc(e_loaded, 16)
                sp.dma_start(w_e[:, :, X_B1:X_B2], a["exp_b1"]).then_inc(e_loaded, 16)
                sp.dma_start(w_e[:, :, X_B2:EXPERT],
                             a["exp_b2"].rearrange("(o e) n -> o e n", o=1).broadcast_to((P, E, P))).then_inc(e_loaded, 16)

            def slot(s):
                if isinstance(s.i, int) and 4 * s.i + s.b == 2:
                    load_experts()
                if not s.odd and s.pair(8):
                    j = s.pair(8)
                    if not isinstance(j.v, int) or j.v >= 2:
                        load_x(j)
                if not s.odd:
                    if s.pair(2):
                        load_stack(s.pair(2))
                    if s.pair(2) and not (isinstance(s.i, int) and s.pair(2).v == 0):
                        load_mask(s.pair(2))
                if s.batch(-2) and not (isinstance(s.i, int) and s.batch(-2).v < 2):
                    load_bias(s.batch(-2))
                if s.odd and s.pair(3):
                    store_parts(s.pair(3))

            all_slots(sp, slot)
            sp.wait_ge(t_tab, 2)
            for e in range(PADS_SP, E):
                first = sp.value_load(pad_i[0:1, e:e + 1], min_val=0, max_val=E * REGION - P)
                sp.dma_start(rows_scr[bass.ds(first, P), :], zero_row[:, :]).then_inc(z_rows_sp, 16)
            for r in range(2):
                sp.wait_ge(g_rows[r], 32 * NB // 2)
            sp.wait_ge(z_rows, 16 * PADS_POOL)
            sp.wait_ge(z_rows_sp, 16 * (E - PADS_SP))
            sp.wait_ge(z_rows_act, 16 * (PADS_SP - PADS_POOL))
            sp.wait_ge(t_tab, TAB_STEPS)

            def load_rows(n):
                wait(sp, mp_t, n.v - 3)
                settle(sp, n)
                wait(sp, mv_meta, n.v - 3)
                settle(sp, n)
                first = sp.value_load(tab[0:1, 1, bass.ds(n.v, 1)], min_val=0, max_val=E * REGION - P)
                sp.dma_start(rows_in[:, n.ring(4)], rows_scr[bass.ds(first, P), :]).then_inc(rows_loaded[n.ring(4)], 16)

            load_rows(At(4, 0, 0, TILES))
            load_rows(At(4, 0, 1, TILES))

            def tile_slot(s):
                if s.tile(-2):
                    load_rows(s.tile(-2))

            all_tiles(sp, tile_slot)

            for r in range(4):
                sp.wait_ge(y_out[r], 16 * TILES // 4)
            for c in range(4):
                for k in range(TOPK):
                    r0 = k * TOKENS + c * 8 * P
                    sp.dma_start(score[:, c, 8 * k:8 * k + 8, :],
                                 y_scr[r0:r0 + 8 * P, :].rearrange("(b t) d -> t b d", t=P)).then_inc(y_loaded[c], 16)
            for c in range(4):
                sp.wait_ge(summed, 2 * c + 2)
                sp.dma_start(out[8 * c:8 * c + 8].rearrange("b t d -> t b d"),
                             resid[:, 8 * c:8 * c + 8, :]).then_inc(stored, 16)
            sp.wait_ge(stored, 16 * 4)

        @block.gpsimd
        def _(pool):
            def step(ins, n):
                ins.then_inc(const_ready, 1)
                pool.wait_ge(const_ready, n)

            step(nc.gpsimd.memset(ident[:], 0.0), 1)
            step(nc.gpsimd.affine_select(out=ident[:], in_=ident[:], compare_op=ALU.not_equal, fill=1.0, base=0,
                                         pattern=[[-1, P]], channel_multiplier=1), 2)
            step(nc.gpsimd.tensor_copy(ident_b[:], ident[:]), 3)
            step(nc.gpsimd.memset(ones_b[:], 1.0), 4)
            step(nc.gpsimd.affine_select(out=before[:], in_=ones_b[:], compare_op=ALU.is_gt, fill=0.0, base=0,
                                         pattern=[[1, P]], channel_multiplier=-1), 5)
            step(nc.gpsimd.memset(m_half[:], -0.5), 6)
            step(nc.gpsimd.iota(iota_e[:], pattern=[[1, E]], base=0, channel_multiplier=0,
                                allow_small_or_imprecise_dtypes=True), 7)
            step(nc.gpsimd.iota(iota_p[:], pattern=[[0, 1]], base=0, channel_multiplier=1,
                                allow_small_or_imprecise_dtypes=True), 8)
            step(nc.gpsimd.iota(dest_tab[:], pattern=[[P, NB], [TOKENS, TOPK]], base=0, channel_multiplier=1,
                                allow_small_or_imprecise_dtypes=True), 9)
            step(nc.gpsimd.iota(count[:], pattern=[[REGION, E]], base=0, channel_multiplier=0,
                                allow_small_or_imprecise_dtypes=True), 10)

            step(nc.gpsimd.iota(base_e[:], pattern=[[-(REGION // P), E]], base=0, channel_multiplier=0,
                                allow_small_or_imprecise_dtypes=True), 11)
            step(nc.gpsimd.memset(run[:], 0.0), 12)
            step(nc.gpsimd.memset(zero_row[:], 0.0), 13)
            step(nc.gpsimd.memset(zero_row[:, DEST:DEST + 1], float(NOWHERE)), 14)
            def sub(n, half):
                pool.wait_ge(v_s, 4 * n.v + 2 * half + 2)
                h0 = 8 * half
                sl = score[:, n.ring(4), h0:h0 + 8, :]
                nc.gpsimd.tensor_tensor(sl, sl, top[:, n.ring(2), h0:h0 + 8].unsqueeze(2).broadcast_to((P, 8, P)),
                                        ALU.subtract).then_inc(g_sub, 1)

            def slot(s):
                n = s.batch(3)
                if n:
                    pool.wait_ge(v_x2, 4 * n.v + 4)
                    nc.gpsimd.tensor_tensor(rs_2[:, n.ring(2):n.ring(2) + 1], mv_2[:, n.ring(2), 1:2], m_half[:, 0:1],
                                            ALU.pow).then_inc(g_r2, 1)
                if s.batch(1):
                    sub(s.batch(1), 1)
                if n:
                    wait(pool, v_x3, 4 * (n.v - 1) + 1)
                    nc.gpsimd.tensor_tensor(x_2b[:], res(n), b2_bc, ALU.add).then_inc(g_b2, 1)
                n = s.batch(4)
                if n:
                    pool.wait_ge(v_x3, 4 * n.v + 4)
                    nc.gpsimd.tensor_tensor(rs_3[:, n.ring(2):n.ring(2) + 1], mv_3[:, n.ring(2), 1:2], m_half[:, 0:1],
                                            ALU.pow).then_inc(g_r3, 1)
                n = s.batch(7)
                if n:
                    pool.wait_ge(v_gates, 2 * n.v + 2)
                    pool.wait_ge(v_pos, 2 * n.v + 2)
                    settle(pool, n)
                    for k in range(TOPK):
                        nc.gpsimd.indirect_dma_start(
                            rows_scr[:, :], bass.IndirectOffsetOnAxis(ap=slot_i[:, n.ring(2), k:k + 1], axis=0),
                            row[:, n.ring(2), k, :], None).then_inc(g_rows[n.ring(2)], 16)
                if s.batch(0):
                    sub(s.batch(0), 0)
                n = s.batch(4)
                if n:
                    pool.wait_ge(v_statt, 3 * n.v + 3)
                    nc.gpsimd.tensor_tensor(rs_t[:, n.ring(2):n.ring(2) + 1], mv_t[:, n.ring(2), 1:2], m_half[:, 0:1],
                                            ALU.pow).then_inc(g_rt, 1)
                if not s.odd and s.pair(6):
                    j = s.pair(6)
                    pool.wait_ge(v_statf, 4 * j.v + 4)
                    nc.gpsimd.tensor_tensor(rs_f[:, j.ring(2)], mv_f[:, j.ring(2), :, 1], m_half[:, 0:2],
                                            ALU.pow).then_inc(g_rf, 1)

            for c in (0, ):
                j = At(2, 0, c)
                pool.wait_ge(v_statf, 4 * j.v + 4)
                nc.gpsimd.tensor_tensor(rs_f[:, j.ring(2)], mv_f[:, j.ring(2), :, 1], m_half[:, 0:2],
                                        ALU.pow).then_inc(g_rf, 1)
            for hh in range(2):
                for r in range(2):
                    step(nc.gpsimd.memset(k_st[64 * hh:64 * hh + 64, r, 1 - hh].rearrange("p a t -> p (a t)").bitcast(U32),
                                          0), 15 + 2 * hh + r)
            step(nc.gpsimd.memset(v_pad[:].rearrange("p r t h c -> p (r t h c)"), 0.0), 19)
            for k in range(8):
                step(nc.gpsimd.memset(bass.AP(tensor=v_pad, offset=k * 8 * VW + HD,
                                              ap=[[4 * 2 * 8 * VW, P], [VW + VC, 8], [1, 1]]), 1.0), 20 + k)

            all_slots(pool, slot)

            pool.wait_ge(t_tab, 2)
            for e in range(PADS_POOL):
                nc.gpsimd.indirect_dma_start(rows_scr[:, :], bass.IndirectOffsetOnAxis(ap=pad_i[:, e:e + 1], axis=0),
                                             zero_row[:, :], None).then_inc(z_rows, 16)

            def tile_slot(s):
                n = s.tile(3)
                if n:
                    pool.wait_ge(ma_y, n.v + 1)
                    settle(pool, n)
                    nc.gpsimd.indirect_dma_start(
                        y_scr[:, :], bass.IndirectOffsetOnAxis(ap=dest_i[:, n.ring(4):n.ring(4) + 1], axis=0),
                        y_g[:, n.ring(4)], None, bounds_check=TOPK * TOKENS - 1,
                        oob_is_err=False).then_inc(y_out[n.ring(4)], 16)

            all_tiles(pool, tile_slot)

        @block.scalar
        def _(act):
            def once(ins):
                ins.then_inc(pre_act, 1)

            act.wait_ge(pre_dve, 9)
            once(nc.scalar.activation(pre[:, 5], pre[:, 4], ACT.Sin))
            act.wait_ge(pre_act, 1)
            once(nc.scalar.activation(pre[:, 6], pre[:, 5], ACT.Silu))
            act.wait_ge(pre_pe, 2)
            once(nc.scalar.activation(shift[:], m1[:, 0:NB], ACT.Identity, bias=cols[:, C_BADA_H:C_BADA_H + 1]))

            def style_1():
                act.wait_ge(pre_pe, 4)
                once(nc.scalar.activation(pre[:, 7], t_ps[0][:, 0:NB], ACT.Relu, bias=cols[:, C_HB1:C_HB1 + 1]))

            def style_2():
                act.wait_ge(pre_pe, 5)
                once(nc.scalar.activation(pre[:, 8], t_ps[1][:, 0:NB], ACT.Identity, bias=cols[:, C_HB2:C_HB2 + 1]))

            def style_3():
                act.wait_ge(pre_pe, 6)
                once(nc.scalar.activation(pre[0:64, 9], c_ps[0:64, 0:NB], ACT.Relu, bias=cols[0:64, C_SB1:C_SB1 + 1]))

            def style_4():
                act.wait_ge(pre_pe, 8)
                once(nc.scalar.activation(beta[:], t_ps[1][:, 0:NB], ACT.Identity, bias=cols[:, C_SB2B:C_SB2B + 1]))

            def style_5():
                act.wait_ge(style_dve, 4)
                once(nc.scalar.activation(pre[:, 10], pre[:, 1], ACT.Exp))
                act.wait_ge(pre_act, 8)
                once(nc.scalar.activation(pre[:, 11], pre[:, 10], ACT.Ln, bias=1.0))

            def exps(n, c):
                act.wait_ge(p_t, 4 * n.v + c + 1)
                wait(act, p_pv, 4 * n.v + c - 1)
                nc.scalar.activation(prob[:, c % 2], t_ps[c % 2][:, :], ACT.Exp).then_inc(a_exp, 1)

            def slot(s):
                n = s.batch(2)
                if n:
                    act.wait_ge(p_pv, 4 * n.v + 4)
                    wait(act, p_den, n.v)
                    nc.scalar.activation(ctx_u[:, :], c_ps[0:VW, 0:2 * P], ACT.Copy).then_inc(a_c, 1)
                n = s.batch(6)
                if n:
                    act.wait_ge(p_rr, n.v + 1)
                    wait(act, g_rows[n.ring(2)], 32 * n.turn(2))
                    nc.scalar.activation(row[:, n.ring(2), :, 0:P + E],
                                         m0[:, 0:P + E].unsqueeze(1).broadcast_to((P, TOPK, P + E)),
                                         ACT.Copy).then_inc(a_rr, 1)
                p = s.batch(1)
                if p:
                    exps(p, 0)
                if not s.odd and s.pair(4):
                    j = s.pair(4)
                    act.wait_ge(p_xt, j.v + 1)
                    wait(act, p_v, j.v - 1)
                    act.wait_ge(pre_act, 3)
                    act.wait_ge(pre_dve, 10)
                    for b in range(2):
                        nc.scalar.activation(x_t[:, j.ring(2), b * P:(b + 1) * P], m0[:, b * P:(b + 1) * P],
                                             ACT.Identity, bias=shift[:, bass.ds(j.v * 2 + b, 1)],
                                             scale=scale1[:, bass.ds(j.v * 2 + b, 1)]).then_inc(a_xt, 1)
                if s.odd and s.pair(3):
                    j = s.pair(3)
                    act.wait_ge(p_qk, j.v + 1)
                    act.wait_ge(pre_dve, 11)
                    wait(act, v_part, 4 * j.v)
                    nc.scalar.activation(qk_f[:, 0:2 * P], m0[:, 0:2 * P], ACT.Identity,
                                         bias=cols[:, C_BQ:C_BQ + 1], scale=float(HD) ** -0.5).then_inc(a_qk, 1)
                    nc.scalar.activation(qk_f[:, 2 * P:4 * P], m0[:, 2 * P:4 * P], ACT.Identity,
                                         bias=cols[:, C_BK:C_BK + 1]).then_inc(a_qk, 1)
                    act.wait_ge(a_qk, 2 * j.v + 2)
                    wait(act, parts_stored, 32 * j.v)
                    nc.scalar.activation(qk_p[:, 0].rearrange("p a t -> p (a t)"), qk_f[:], ACT.Copy).then_inc(a_part, 1)
                n = s.batch(3)
                if n:
                    act.wait_ge(p_n2, n.v + 1)
                    wait(act, p_up, n.v)
                    nc.scalar.activation(h_2[:], m2[:, 0:P], ACT.Identity, bias=cols[:, C_BETA2:C_BETA2 + 1],
                                         scale=cols[:, C_G2:C_G2 + 1]).then_inc(a_h2, 1)
                if p:
                    exps(p, 1)
                n = s.batch(2)
                if n:
                    act.wait_ge(p_ct, n.v + 1)
                    wait(act, p_wo, n.v)
                    nc.scalar.activation(ctx_t[:], m1[:, 0:P], ACT.Copy).then_inc(a_ct, 1)
                n = s.batch(3)
                if n:
                    act.wait_ge(p_up, n.v + 1)
                    wait(act, v_gelu, n.v)
                    nc.scalar.activation(up_t[:], m2[:, :].rearrange("p (c t) -> p c t", c=NCH), ACT.Tanh,
                                         scale=0.851).then_inc(a_tanh, 1)
                n = s.batch(5)
                if n:
                    act.wait_ge(v_hf, n.v + 1)
                    wait(act, p_rr, n.v)
                    nc.scalar.activation(h_f[:], h_t[:, n.ring(2)], ACT.Identity, bias=coef[:, 2:3],
                                         scale=coef[:, 0:1]).then_inc(a_hf, 1)
                if p:
                    exps(p, 2)
                n = s.batch(4)
                if n:
                    act.wait_ge(p_zt, n.v + 1)
                    nc.scalar.activation(h_t[:, n.ring(2)], m0[:, 0:P], ACT.Identity, bias=cols[:, C_LNB:C_LNB + 1],
                                         scale=cols[:, C_LNG:C_LNG + 1]).then_inc(a_ht, 1)
                n = s.batch(6)
                if n:
                    act.wait_ge(v_route, 3 * n.v + 2)
                    nc.scalar.activation(gate[:, 1:2], gate[:, 0:1], ACT.Tanh, scale=0.5).then_inc(a_gate, 1)
                if s.odd and s.pair(1):
                    j = s.pair(1)
                    act.wait_ge(mask_loaded[j.ring(2)], 16 * (j.turn(2) + 1))
                    wait(act, p_s, 8 * (j.v - 1))
                    nc.scalar.activation(mask_b[:, j.ring(2)], mask_u8[:, j.ring(2)], ACT.Copy,
                                         scale=MASKED).then_inc(a_mask, 1)
                if p:
                    exps(p, 3)

            all_slots(act, slot, {-3: style_1, -2: style_2, -1: style_3, 0: style_4, 1: style_5})

            act.wait_ge(t_tab, 2)
            for e in range(PADS_POOL, PADS_SP):
                first = act.value_load(pad_i[0:1, e:e + 1], min_val=0, max_val=E * REGION - P)
                act.dma_start(rows_scr[bass.ds(first, P), :], zero_row[:, :]).then_inc(z_rows_act, 16)
            act.wait_ge(t_tab, TAB_STEPS)

            def tile_slot(s):
                n = s.tile(0)
                if n:
                    act.wait_ge(mp_t, n.v + 1)
                    wait(act, mp_up, n.v - 1)
                    nc.scalar.activation(h_mt[:, n.ring(2)], t_ps[n.ring(2)][:, 0:P], ACT.Copy).then_inc(ma_ht, 1)
                n = s.tile(1)
                if n:
                    act.wait_ge(mp_up, n.v + 1)
                    wait(act, mp_dn, n.v - 1)
                    for c in range(NCH):
                        ins = nc.scalar.activation(hid[:, n.ring(2), c], s_ps[n.ring(2)][:, c * P:(c + 1) * P], ACT.Relu,
                                                   bias=w_now[n.ring(4)][:, X_B1 + c:X_B1 + c + 1])
                    ins.then_inc(ma_relu, 1)
                n = s.tile(2)
                if n:
                    act.wait_ge(mv_y, n.v + 1)
                    wait(act, y_out[n.ring(4)], 16 * n.turn(4))
                    nc.scalar.activation(y_g[:, n.ring(4)], y_b[:, n.ring(2)], ACT.Copy,
                                         scale=gate_m[:, n.ring(4):n.ring(4) + 1]).then_inc(ma_y, 1)

            all_tiles(act, tile_slot)

        @block.vector
        def _(dve):
            seen = [0]

            def once(ins):
                ins.then_inc(pre_dve, 1)
                seen[0] += 1
                dve.wait_ge(pre_dve, seen[0])

            def stats_f(j, between=()):
                r = j.ring(2)
                dve.wait_ge(x_loaded[r], 16 * (j.turn(2) + 1))
                settle(dve, j)
                for b in range(2):
                    nc.vector.bn_stats(stat_f[:, b], x_in[:, r, b]).then_inc(v_statf, 1)
                dve.wait_ge(v_statf, 4 * j.v + 2)
                settle(dve, j)
                for b in range(2):
                    nc.vector.bn_aggr(mv_f[:, r, b], stat_f[:, b]).then_inc(v_mv, 1)
                while between:
                    between.pop(0)()
                dve.wait_ge(v_mv, 2 * j.v + 2)
                wait(dve, g_rf, j.v - 1)
                nc.vector.tensor_scalar(mv_f[:, r, :, 1], mv_f[:, r, :, 1], EPS, None, ALU.add).then_inc(v_statf, 2)

            stats_f(At(2, 0, 0))

            dve.wait_ge(c_loaded, 16 * N_C)
            dve.wait_ge(const_ready, 10)
            once(nc.vector.tensor_copy(pre[:, 0], ints[:, 0]))
            once(nc.vector.tensor_scalar(pre[:, 0], pre[:, 0], 0.01, 4000.0, ALU.mult, ALU.mult))
            once(nc.vector.tensor_scalar(pre[:, 1], pre[:, 0], cols[:, C_FREQ:C_FREQ + 1], None, ALU.mult))
            two_pi = 2 * np.pi
            c1 = 6.28125
            c2 = float(np.float32(np.floor((two_pi - c1) * 2 ** 20) / 2 ** 20))
            c3 = float(np.float32(two_pi - c1 - c2))
            magic = 1.5 * 2 ** 23
            once(nc.vector.tensor_scalar(pre[:, 2], pre[:, 1], 1.0 / two_pi, cols[:, C_PHASE:C_PHASE + 1],
                                         ALU.mult, ALU.add))
            once(nc.vector.tensor_scalar(pre[:, 2], pre[:, 2], magic, magic, ALU.add, ALU.subtract))
            once(nc.vector.scalar_tensor_tensor(pre[:, 3], pre[:, 2], -c1, pre[:, 1], ALU.mult, ALU.add))
            once(nc.vector.scalar_tensor_tensor(pre[:, 4], pre[:, 2], -c2, pre[:, 3], ALU.mult, ALU.add))
            once(nc.vector.scalar_tensor_tensor(pre[:, 3], pre[:, 2], -c3, pre[:, 4], ALU.mult, ALU.add))
            dve.wait_ge(pre_dve, 8)
            nc.vector.tensor_scalar(pre[:, 2], cols[:, C_PHASE:C_PHASE + 1].broadcast_to((P, NB)), two_pi, None,
                                    ALU.mult).then_inc(dve_const, 1)
            dve.wait_ge(dve_const, 1)
            nc.vector.tensor_tensor(pre[:, 4], pre[:, 3], pre[:, 2], ALU.add).then_inc(dve_const, 1)
            dve.wait_ge(dve_const, 2)
            once(nc.vector.tensor_scalar(pre[:, 4], pre[:, 4], float(np.float32(3.1415925)),
                                         -float(np.float32(3.1415925)), ALU.min, ALU.max))
            dve.wait_ge(pre_pe, 1)
            once(nc.vector.tensor_scalar(scale1[:], m0[:, 0:NB], cols[:, C_BADA_S:C_BADA_S + 1], 1.0,
                                         ALU.add, ALU.add))
            once(nc.vector.tensor_scalar(cols[:, C_BQ:C_BQ + 1], cols[:, C_BQ:C_BQ + 1], float(HD) ** -0.5, None,
                                         ALU.mult))
            once(nc.vector.tensor_scalar(pre[0:NB, 2], ints[0:NB, 1], iota_p[0:NB, 0:1], None, ALU.is_equal))

            styled = [0]

            def style(ins):
                styled[0] += 1
                ins.then_inc(style_dve, 1)
                dve.wait_ge(style_dve, styled[0])

            def style_0():
                dve.wait_ge(pre_pe, 3)
                style(nc.vector.tensor_copy(pre[0:64, 3], c_ps[0:64, 0:NB]))

            def style_4():
                dve.wait_ge(pre_pe, 7)
                style(nc.vector.tensor_scalar(gamma[:, :, 0], t_ps[0][:, 0:NB], cols[:, C_SB2G:C_SB2G + 1], None,
                                              ALU.add))
                style(nc.vector.tensor_scalar(pre[:, 0], gamma[:, :, 0], -1.0, None, ALU.mult))
                style(nc.vector.tensor_tensor(pre[:, 1], pre[:, 0], gamma[:, :, 0], ALU.min))

            def style_5():
                dve.wait_ge(pre_act, 9)
                style(nc.vector.scalar_tensor_tensor(gamma[:, :, 0], gamma[:, :, 0], 0.0, pre[:, 11],
                                                     ALU.max, ALU.add))
                style(nc.vector.tensor_scalar(gamma[:, :, 0], gamma[:, :, 0], EPS_T, None, ALU.add))
                style(nc.vector.tensor_scalar(gamma[:, :, 1], gamma[:, :, 0], -1.0, None, ALU.mult))

            def norm_f(j):
                r = j.ring(2)
                dve.wait_ge(g_rf, j.v + 1)
                wait(dve, p_xt, j.v)
                for b in range(2):
                    nc.vector.tensor_scalar(x_n[:, b], x_in[:, r, b], mv_f[:, r, b, 0:1], rs_f[:, r, b:b + 1],
                                            ALU.subtract, ALU.mult).then_inc(v_xn, 1)

            def scores(n, c, *between):
                between = list(between) + [None] * (4 - len(between))
                if n:
                    if c == 0:
                        dve.wait_ge(bias_loaded[n.ring(4)], 32 * (n.turn(4) + 1))
                        wait(dve, g_sub, 2 * (n.v - 1))
                    dve.wait_ge(p_s, 4 * n.v + c + 1)
                    settle(dve, n)
                for k, step in enumerate(between):
                    if n:
                        h = 4 * c + k
                        ins = nc.vector.tensor_tensor_reduce(
                            score[:, n.ring(4), h, :], s_ps[c % 2][:, k * P:(k + 1) * P], score[:, n.ring(4), h, :],
                            1.0, -3.4e38, ALU.add, ALU.max, top[:, n.ring(2), h:h + 1])
                        if k == 3:
                            ins.then_inc(v_s, 1)
                    if step:
                        step()

            def stats(n, src, st, mv, eps, s_, k):
                if not n:
                    return ()

                def first():
                    if k == 4:
                        dve.wait_ge(s_, k * n.v + 1)
                        settle(dve, n)
                    nc.vector.bn_stats(st[:], src).then_inc(s_, 1)

                def second():
                    dve.wait_ge(s_, k * n.v + k - 2)
                    settle(dve, n)
                    nc.vector.bn_aggr(mv[:, n.ring(2)], st[:]).then_inc(s_, 1)

                def third():
                    dve.wait_ge(s_, k * n.v + k - 1)
                    nc.vector.tensor_scalar(mv[:, n.ring(2), 1:2], mv[:, n.ring(2), 1:2], eps, None,
                                            ALU.add).then_inc(s_, 1)

                return first, second, third

            norm_f(At(2, 0, 0))

            made = [0]

            def make(ins):
                made[0] += 1
                ins.then_inc(b1_ready, 1)
                dve.wait_ge(b1_ready, made[0])

            def b1_part(k):
                rows = slice(32 * k, 32 * k + NCH)
                if k == 0:
                    dve.wait_ge(w_loaded, 16 * N_W)
                    make(nc.vector.memset(b1_p[:], 0.0))
                    make(nc.vector.memset(sel[:], 0.0))
                src = b1_f[rows]
                for m in range(k):
                    make(nc.vector.tensor_copy(b1_t[rows, m], src))
                    make(nc.vector.tensor_tensor(b1_r[rows, m], src, b1_t[rows, m], ALU.subtract))
                    src = b1_r[rows, m]
                make(nc.vector.tensor_copy(b1_p[rows], src))
                make(nc.vector.tensor_copy(sel[rows], ident_b[rows, rows].unsqueeze(2).broadcast_to((NCH, NCH, P))))

            def slot(s):
                n = s.batch(7)
                if n:
                    dve.wait_ge(p_pos, n.v + 1)
                    nc.vector.tensor_tensor(pos[:], m1[:, 0:E], count[:], ALU.add).then_inc(v_posc, 1)
                n = s.batch(4)
                if n:
                    dve.wait_ge(p_dn, n.v + 1)
                    dve.wait_ge(g_b2, n.v + 1)
                    wait(dve, v_z, n.v)
                    nc.vector.scalar_tensor_tensor(res(n), m2[:, 0:P], 0.5,
                                                   x_2b[:], ALU.mult, ALU.add).then_inc(v_x3, 1)
                n = s.batch(7)
                if n:
                    dve.wait_ge(v_posc, 5 * n.v + 1)
                    nc.vector.tensor_tensor(count[:], m1[:, E:2 * E], count[:], ALU.add).then_inc(v_pos, 1)
                n = s.batch(4)
                scores(s.batch(0), 0, *(stats(n, res(n), stat_3, mv_3, EPS, v_x3, 4) if n else ()))
                n = s.batch(3)
                if n:
                    dve.wait_ge(g_r2, n.v + 1)
                    wait(dve, p_n2, n.v)
                    nc.vector.tensor_scalar(n_2[:], res(n), mv_2[:, n.ring(2), 0:1],
                                            rs_2[:, n.ring(2):n.ring(2) + 1], ALU.subtract, ALU.mult).then_inc(v_n2, 1)
                n = s.batch(7)
                if n:
                    dve.wait_ge(a_gate, n.v + 1)
                    wait(dve, g_rows[n.ring(2)], 32 * n.turn(2))
                    for k in range(TOPK):
                        nc.vector.tensor_scalar(row[:, n.ring(2), k, GATE:GATE + 1], gate[:, 1:2], k - 0.5, 0.5,
                                                ALU.mult, ALU.add).then_inc(v_gates, 1)
                n = s.batch(2)
                if n:
                    dve.wait_ge(p_den, n.v + 1)
                    c9 = m1[:, 0:2 * VW].rearrange("p (h c) -> p h c", c=VC)
                    nc.vector.reciprocal(r_den[:], c9[:, :, HD]).then_inc(v_ctx, 1)
                    dve.wait_ge(v_ctx, 2 * n.v + 1)
                    wait(dve, p_ct, n.v)
                    nc.vector.tensor_tensor(ctx_n[:].rearrange("p (h d) -> p h d", d=HD), c9[:, :, 0:HD],
                                            r_den[:].unsqueeze(2).broadcast_to((P, H, HD)), ALU.mult).then_inc(v_ctx, 1)
                n = s.batch(7)
                if n:
                    hot_n = hot[:, n.ring(2)]

                    def pick_rows(n=n, hot_n=hot_n):
                        nc.vector.tensor_tensor(pick[:], hot_n, pos[:].unsqueeze(1).broadcast_to((P, TOPK, E)),
                                                ALU.mult).then_inc(v_posc, 1)

                    def sum_rows(n=n):
                        dve.wait_ge(v_posc, 5 * n.v + 2)
                        nc.vector.tensor_reduce(slot_f[:], pick[:], AX.X, ALU.add).then_inc(v_posc, 1)

                    def put_dest(n=n):
                        nc.vector.tensor_copy(row[:, n.ring(2), :, DEST],
                                              dest_tab[:, bass.ds(n.v, 1), :]).then_inc(v_posc, 2)

                    def put_rows(n=n):
                        dve.wait_ge(v_posc, 5 * n.v + 5)
                        nc.vector.tensor_copy(slot_i[:, n.ring(2)], slot_f[:]).then_inc(v_pos, 1)

                    scores(s.batch(0), 1, pick_rows, sum_rows, put_dest, put_rows)
                else:
                    scores(s.batch(0), 1)
                if not s.odd and s.pair(4):
                    j = s.pair(4)
                    dve.wait_ge(p_xb, j.v + 1)
                    nc.vector.tensor_tensor(resid[:, bass.ds(j.v * 2, 2), :],
                                            m0[:, 0:2 * P].rearrange("p (b d) -> p b d", b=2),
                                            bo_bc.unsqueeze(1).broadcast_to((P, 2, P)), ALU.add).then_inc(v_xb, 1)
                if s.odd and s.pair(1):
                    j = s.pair(1)
                    dve.wait_ge(p_v, j.v + 1)
                    if isinstance(j.v, int) and j.v == 0:
                        dve.wait_ge(const_ready, CONSTS)
                    for b in range(2):
                        r = (2 * j.c + b) % 4
                        wait(dve, p_pv, 4 * (j.v * 2 + b - 3))
                        dst = bass.AP(tensor=v_pad, offset=r * 2 * 8 * VW,
                                      ap=[[4 * 2 * 8 * VW, P], [8 * VW, 2], [VW + VC, 8], [1, HD]])
                        nc.vector.tensor_tensor(dst, m0[:, b * P:(b + 1) * P].rearrange("p (t h d) -> p t h d", t=2, d=HD),
                                                bv_bc.rearrange("p (t h d) -> p t h d", t=2, d=HD),
                                                ALU.add).then_inc(v_v, 1)
                n = s.batch(5)
                if n:
                    r = n.ring(2)
                    dve.wait_ge(g_rt, n.v + 1)
                    b_n = beta[:, bass.ds(n.v, 1)]
                    wait(dve, a_hf, n.v)
                    nc.vector.tensor_tensor(coef[:, 0:2], gamma[:, bass.ds(n.v, 1), :].rearrange("p o k -> p (o k)"),
                                            rs_t[:, r:r + 1].broadcast_to((P, 2)), ALU.mult).then_inc(v_hf3, 1)
                    dve.wait_ge(v_hf3, n.v + 1)
                    nc.vector.scalar_tensor_tensor(coef[:, 2:3], mv_t[:, r, 0:1], coef[:, 1:2], b_n,
                                                   ALU.mult, ALU.add).then_inc(v_hf, 1)
                n = s.batch(4)
                if n:
                    dve.wait_ge(g_r3, n.v + 1)
                    wait(dve, p_zt, n.v)
                    nc.vector.tensor_scalar(z_3[:], res(n), mv_3[:, n.ring(2), 0:1],
                                            rs_3[:, n.ring(2):n.ring(2) + 1], ALU.subtract, ALU.mult).then_inc(v_z, 1)
                n = s.batch(6)
                if n:
                    lg = row[:, n.ring(2), 0, P:P + E]
                    dve.wait_ge(a_rr, n.v + 1)
                    settle(dve, n)
                    nc.vector.max(top8[:], lg).then_inc(v_rt, 1)

                    def find(n=n, lg=lg):
                        dve.wait_ge(v_rt, 4 * n.v + 1)
                        settle(dve, n)
                        nc.vector.max_index(ix8[:], top8[:], lg).then_inc(v_rt, 1)
                        wait(dve, a_gate, n.v)
                        nc.vector.tensor_tensor(gate[:, 0:1], top8[:, 1:2], top8[:, 0:1],
                                                ALU.subtract).then_inc(v_route, 2)

                    def to_float(n=n):
                        dve.wait_ge(v_rt, 4 * n.v + 2)
                        nc.vector.tensor_copy(ix_f[:], ix8[:, 0:TOPK]).then_inc(v_rt, 1)

                    def one_hot(n=n):
                        dve.wait_ge(v_rt, 4 * n.v + 3)
                        nc.vector.tensor_tensor(hot[:, n.ring(2)], ix_f[:].unsqueeze(2).broadcast_to((P, TOPK, E)),
                                                iota_e[:].unsqueeze(1).broadcast_to((P, TOPK, E)),
                                                ALU.is_equal).then_inc(v_rt, 1)

                    def both_hot(n=n):
                        dve.wait_ge(v_rt, 4 * n.v + 4)
                        wait(dve, p_pos, n.v)
                        nc.vector.tensor_tensor(hot_b[:], hot[:, n.ring(2), 0], hot[:, n.ring(2), 1],
                                                ALU.add).then_inc(v_route, 1)

                    scores(s.batch(0), 2, find, to_float, one_hot, both_hot)
                else:
                    scores(s.batch(0), 2)
                n = s.batch(3)
                if n:
                    dve.wait_ge(a_tanh, n.v + 1)
                    wait(dve, p_dn, n.v)
                    nc.vector.scalar_tensor_tensor(act_1[:], up_t[:], 1.0,
                                                   m2[:, :].rearrange("p (c t) -> p c t", c=NCH),
                                                   ALU.add, ALU.mult).then_inc(v_gelu, 1)
                if s.odd and s.pair(5):
                    norm_f(s.pair(5))
                if s.odd and s.pair(3):
                    j = s.pair(3)
                    dve.wait_ge(a_part, j.v + 1)
                    flat = [qk_p[:, k].rearrange("p a t -> p (a t)") for k in range(3)]
                    nc.vector.tensor_tensor(qk_r[:], qk_f[:], flat[0], ALU.subtract).then_inc(v_part, 2)
                n = s.batch(2)
                if n:
                    dve.wait_ge(p_wo, n.v + 1)
                    nc.vector.tensor_tensor(res(n), m1[:, 0:P], res(n),
                                            ALU.add).then_inc(v_x2, 1)
                scores(s.batch(0), 3, *(stats(n, res(n), stat_2, mv_2, EPS, v_x2, 4) if n else ()))
                if s.odd and s.pair(3):
                    dve.wait_ge(v_part, 4 * j.v + 2)
                    nc.vector.tensor_copy(flat[1], qk_r[:]).then_inc(v_part, 1)
                    dve.wait_ge(v_part, 4 * j.v + 3)
                    nc.vector.tensor_tensor(flat[2], qk_r[:], flat[1], ALU.subtract).then_inc(v_part, 1)
                n = s.batch(4)
                if n:
                    dve.wait_ge(a_ht, n.v + 1)
                    settle(dve, n)
                chain = list(stats(n, h_t[:, n.ring(2)], stat_t, mv_t, EPS_T, v_statt, 3)) if n else []
                if chain:
                    chain.pop(0)()
                if not s.odd and s.pair(6):
                    stats_f(s.pair(6), chain)
                for step in chain:
                    step()

            def tile_rounding():
                dve.wait_ge(const_ready, 11)
                nc.vector.tensor_scalar(base_e[:], base_e[:], 0.5 - 0.5 / P, None, ALU.add).then_inc(dve_const, 1)

            all_slots(dve, slot, {-4: lambda: (style_0(), tile_rounding()), -2: lambda: b1_part(0), -1: lambda: b1_part(1),
                                  0: style_4, 1: style_5, 2: lambda: b1_part(2)})

            steps = [0]

            def table(ins, n=1):
                steps[0] += n
                ins.then_inc(t_tab, n)
                dve.wait_ge(t_tab, steps[0])

            V = nc.vector
            dve.wait_ge(v_pos, 2 * NB)
            dve.wait_ge(const_ready, 12)
            table(V.tensor_scalar(pad_f[:], count[:], iota_p[:, 0:1], None, ALU.add))
            table(V.tensor_copy(pad_i[:], pad_f[:]))
            table(V.scalar_tensor_tensor(run[:, 0, 4:], count[:], 1.0 / P, base_e[:], ALU.mult, ALU.add))
            table(V.tensor_scalar(run[:, 0, 4:], run[:, 0, 4:], magic, magic, ALU.add, ALU.subtract))
            for k in range(3):
                table(V.tensor_tensor(run[:, k + 1, 4:], run[:, k, 4:], run[:, k, 4 - 2 ** k:4 + E - 2 ** k], ALU.add))
            table(V.tensor_scalar(past[:, 1], run[:, 0, 4:], -float(P), float(REGION), ALU.mult, ALU.add))
            table(V.tensor_scalar(past[:, 0, 0:E - 1], run[:, 3, 4:3 + E], iota_p[:, 0:1], None, ALU.is_le))
            table(V.tensor_reduce(tc[:, 0:1], past[:, 0, 0:E - 1], AX.X, ALU.add))
            table(V.tensor_tensor(past[:, 2, 0:E - 1], past[:, 0, 0:E - 1], past[:, 1, 0:E - 1], ALU.mult))
            table(V.tensor_reduce(tc[:, 1:2], past[:, 2, 0:E - 1], AX.X, ALU.add))
            table(V.scalar_tensor_tensor(tc[:, 2:3], iota_p[:], float(P), tc[:, 1:2], ALU.mult, ALU.add))
            table(V.tensor_tensor(tc[:, 3:4], tc[:, 2:3], count[:, E - 1:E], ALU.min))
            dve.wait_ge(mp_tab, 1)
            table(V.tensor_copy(tab[:], c_ps[0:1, 0:2 * P].rearrange("p (k t) -> p k t", k=2)))
            assert steps[0] == TAB_STEPS
            dve.wait_ge(e_loaded, 16 * N_E)

            def fetch_expert(n):
                e = dve.value_load(tab[0:1, 0, bass.ds(n.v, 1)], min_val=0, max_val=E - 1)
                wait(dve, mv_y, n.v - 3)
                nc.vector.tensor_copy(w_now[n.ring(4)], w_e[:, bass.ds(e, 1), :].rearrange("p o f -> p (o f)")).then_inc(
                    mv_w, 1)

            fetch_expert(At(4, 0, 0, TILES))

            def tile_slot(s):
                if s.tile(-1):
                    fetch_expert(s.tile(-1))
                n = s.tile(2)
                if n:
                    dve.wait_ge(mp_dn, n.v + 1)
                    wait(dve, ma_y, n.v - 1)
                    nc.vector.tensor_tensor(y_b[:, n.ring(2)], [m0, m1][n.ring(2)][:, 0:P],
                                            w_now[n.ring(4)][:, X_B2:EXPERT], ALU.add).then_inc(mv_y, 1)
                n = s.tile(0)
                if n:
                    r = n.ring(4)
                    dve.wait_ge(rows_loaded[r], 16 * (n.turn(4) + 1))
                    wait(dve, y_out[r], 16 * n.turn(4))
                    nc.vector.tensor_copy(dest_i[:, r:r + 1], rows_in[:, r, DEST:DEST + 1])
                    nc.vector.tensor_copy(gate_m[:, r:r + 1], rows_in[:, r, GATE:GATE + 1]).then_inc(mv_meta, 1)

            all_tiles(dve, tile_slot)

            for c in range(4):
                dve.wait_ge(y_loaded[c], 32)
                for k in range(TOPK):
                    nc.vector.tensor_tensor(resid[:, 8 * c:8 * c + 8, :], resid[:, 8 * c:8 * c + 8, :],
                                            score[:, c, 8 * k:8 * k + 8, :], ALU.add).then_inc(summed, 1)
                    dve.wait_ge(summed, 2 * c + k + 1)

        @block.tensor
        def _(pe):
            mm = nc.tensor.matmul

            pe.wait_ge(c_loaded, 16 * N_C)
            pe.wait_ge(pre_act, 2)
            mm(m0[:, 0:NB], w_ada[:, 0:P], pre[:, 6], start=True, stop=True).then_inc(pre_pe, 1)
            mm(m1[:, 0:NB], w_ada[:, P:2 * P], pre[:, 6], start=True, stop=True).then_inc(pre_pe, 1)
            pe.wait_ge(w_loaded, 16 * N_W)
            pe.wait_ge(pre_dve, 12)
            mm(c_ps[0:64, 0:NB], subj[:], pre[0:NB, 2], start=True, stop=True).then_inc(pre_pe, 1)

            def style_1():
                pe.wait_ge(style_dve, 1)
                mm(t_ps[0][:, 0:NB], hyp_w1, pre[0:64, 3], start=True, stop=True).then_inc(pre_pe, 1)

            def style_2():
                pe.wait_ge(pre_act, 4)
                mm(t_ps[1][:, 0:NB], hyp_w2, pre[:, 7], start=True, stop=True).then_inc(pre_pe, 1)

            def style_3():
                pe.wait_ge(pre_act, 5)
                mm(c_ps[0:64, 0:NB], sty_w1, pre[:, 8], start=True, stop=True).then_inc(pre_pe, 1)
                pe.wait_ge(const_ready, 18)

            def style_4():
                pe.wait_ge(pre_act, 6)
                mm(t_ps[0][:, 0:NB], sty_w2[:, 0:P], pre[0:64, 9], start=True, stop=True).then_inc(pre_pe, 1)
                mm(t_ps[1][:, 0:NB], sty_w2[:, P:2 * P], pre[0:64, 9], start=True, stop=True).then_inc(pre_pe, 1)
                pe.wait_ge(style_dve, 2)
                pe.wait_ge(pre_act, 7)
                pe.wait_ge(const_ready, CONSTS)

            def scores(n, c):
                j_r, b = (n.c // 2) % 2, n.c % 2
                if c == 0:
                    pe.wait_ge(stack_loaded[j_r], 16 * 12 * (n.i + n.c // 4 + 1))
                    pe.wait_ge(a_mask, n.i * 2 + n.c // 2 + 1)
                wait(pe, v_s, 4 * n.v + c - 1)
                ps = s_ps[c % 2]
                mm(ps[:, :], ident_b[:], mask_b[:, j_r, b].unsqueeze(1).broadcast_to((P, 4, P)), start=True, stop=False,
                   skip_group_check=True)
                for k in range(2):
                    pr = 2 * c + k
                    ins = mm(ps[:, k * 2 * P:(k + 1) * 2 * P], q_st[:, j_r, pr, b * P:(b + 1) * P],
                             k_st[:, j_r, :, pr, b * P:(b + 1) * P], start=False, stop=True,
                             skip_group_check=True)
                ins.then_inc(p_s, 1)

            def turn(n, c):
                if c % 2 == 0:
                    pe.wait_ge(g_sub, 2 * n.v + c // 2 + 1)
                wait(pe, a_exp, 4 * n.v + c - 1)
                for k in range(4):
                    ins = pe.transpose(t_ps[c % 2][:, k * P:(k + 1) * P], score[:, n.ring(4), 4 * c + k, :], ident[:])
                ins.then_inc(p_t, 1)

            def values(n, c):
                if c == 0:
                    wait(pe, a_c, n.v)
                    pe.wait_ge(v_v, n.v + 1)
                pe.wait_ge(a_exp, 4 * n.v + c + 1)
                for k in range(4):
                    h = 4 * c + k
                    ins = mm(c_ps[0:VW, (h // 8) * P:(h // 8 + 1) * P], v_pad[:, n.ring(4), h // 8, h % 8, :],
                             prob[:, c % 2, k * P:(k + 1) * P], start=(h % 8 == 0), stop=(h % 8 == 7))
                ins.then_inc(p_pv, 1)

            def slot(s):
                n, p = s.batch(0), s.batch(1)
                if p:
                    turn(p, 0)
                if n:
                    scores(n, 0)
                rr6 = (s.batch(6), a_rr, s.batch(6).v + 1)
                zt5 = (s.batch(5), a_ht, s.batch(5).v + 1)
                if not s.odd and s.pair(4):
                    j = s.pair(4)
                    pe.wait_ge(v_xn, 2 * j.v + 2)
                    wait_first(pe, rr6, zt5, (s.pair(0), v_v, 2 * s.pair(0).v + 2), (s.pair(3), a_qk, 2 * s.pair(2).v + 2))
                    for b in range(2):
                        ins = pe.transpose(m0[:, b * P:(b + 1) * P], x_n[:, b], ident[:])
                    ins.then_inc(p_xt, 1)
                if s.odd and s.pair(3):
                    j = s.pair(3)
                    pe.wait_ge(a_xt, 2 * j.v + 2)
                    wait_first(pe, rr6, zt5, (True, v_xb, s.pair(3).v + 1))
                    mm(m0[:, 0:2 * P], w_q, x_t[:, j.ring(2)], start=True, stop=True)
                    mm(m0[:, 2 * P:4 * P], w_k, x_t[:, j.ring(2)], start=True, stop=True).then_inc(p_qk, 1)
                if s.batch(2):
                    d = s.batch(2)
                    pe.wait_ge(a_c, d.v + 1)
                    wait_first(pe, (s.batch(7), v_pos, 2 * s.batch(7).v + 1), (s.batch(3), v_x2, 4 * s.batch(3).v + 1))
                    for t in range(2):
                        ins = pe.transpose(m1[:, t * VW:(t + 1) * VW], ctx_u[:, t * P:(t + 1) * P], ident[0:VW, 0:VW])
                    ins.then_inc(p_den, 1)
                if p:
                    values(p, 0)
                if s.batch(3):
                    d = s.batch(3)
                    pe.wait_ge(v_n2, d.v + 1)
                    wait(pe, v_x3, 4 * (d.v - 1) + 1)
                    pe.transpose(m2[:, 0:P], n_2[:], ident[:]).then_inc(p_n2, 1)
                if p:
                    turn(p, 1)
                if n:
                    scores(n, 1)
                if not s.odd and s.pair(4):
                    j = s.pair(4)
                    pe.wait_ge(a_xt, 2 * j.v + 2)
                    for b in range(2):
                        ins = pe.transpose(m0[:, b * P:(b + 1) * P], x_t[:, j.ring(2), b * P:(b + 1) * P], ident[:])
                    ins.then_inc(p_xb, 1)
                if s.odd and s.pair(1):
                    j = s.pair(1)
                    wait_first(pe, (s.pair(3), a_qk, 2 * s.pair(3).v + 2), rr6, zt5)
                    for b in range(2):
                        ins = mm(m0[:, b * P:(b + 1) * P], x_t[:, j.ring(2), b * P:(b + 1) * P], w_v,
                                 start=True, stop=True)
                    ins.then_inc(p_v, 1)
                if s.batch(2):
                    d = s.batch(2)
                    pe.wait_ge(v_ctx, 2 * d.v + 2)
                    pe.transpose(m1[:, 0:P], ctx_n[:], ident[:]).then_inc(p_ct, 1)
                if s.batch(3):
                    d = s.batch(3)
                    pe.wait_ge(a_h2, d.v + 1)
                    mm(m2[:, :], b1_p[:], sel[:].rearrange("p c t -> p (c t)"), start=True, stop=False,
                       skip_group_check=True)
                    for c in range(NCH):
                        ins = mm(m2[:, c * P:(c + 1) * P], w_1[:, c * P:(c + 1) * P], h_2[:], start=False, stop=True,
                                 skip_group_check=True)
                    ins.then_inc(p_up, 1)
                if p:
                    values(p, 1)
                if p:
                    turn(p, 2)
                if n:
                    scores(n, 2)
                if s.batch(4):
                    d = s.batch(4)
                    pe.wait_ge(v_z, d.v + 1)
                    wait_first(pe, (not s.odd and s.pair(4), v_xb, s.pair(4).v + 1),
                               (s.odd and s.pair(1), v_v, 2 * s.pair(1).v + 2), rr6, zt5)
                    pe.transpose(m0[:, 0:P], z_3[:], ident[:]).then_inc(p_zt, 1)
                if s.batch(2):
                    d = s.batch(2)
                    pe.wait_ge(a_ct, d.v + 1)
                    mm(m1[:, 0:P], ctx_t[:], w_o, start=True, stop=True).then_inc(p_wo, 1)
                if p:
                    values(p, 2)
                if p:
                    turn(p, 3)
                if n:
                    scores(n, 3)
                if s.batch(5):
                    d = s.batch(5)
                    pe.wait_ge(a_hf, d.v + 1)
                    wait_first(pe, (s.batch(4), a_ht, s.batch(4).v + 1), rr6)
                    pe.transpose(m0[:, 0:P], h_f[:], ident[:])
                    mm(m0[:, P:P + E], h_f[:], w_r, start=True, stop=True).then_inc(p_rr, 1)
                if s.batch(6):
                    d = s.batch(6)
                    pe.wait_ge(v_route, 3 * d.v + 3)
                    wait_first(pe, (s.batch(2), v_x2, 4 * s.batch(2).v + 1), (s.batch(7), v_pos, 2 * s.batch(7).v + 1))
                    mm(m1[:, 0:E], before[:], hot_b[:], start=True, stop=True)
                    mm(m1[:, E:2 * E], ones_b[:], hot_b[:], start=True, stop=True).then_inc(p_pos, 1)
                if s.batch(3):
                    d = s.batch(3)
                    pe.wait_ge(v_gelu, d.v + 1)
                    for c in range(NCH):
                        ins = mm(m2[:, 0:P], act_1[:, c], w_2[:, c], start=(c == 0), stop=(c == NCH - 1))
                    ins.then_inc(p_dn, 1)
                if p:
                    values(p, 3)

            all_slots(pe, slot, {-3: style_1, -2: style_2, -1: style_3, 0: style_4,
                                 2: lambda: pe.wait_ge(b1_ready, B1_STEPS)})

            pe.wait_ge(t_tab, TAB_STEPS - 1)
            mm(c_ps[0:1, 0:P], tc[:, 0:1], ident[:], start=True, stop=True)
            mm(c_ps[0:1, P:2 * P], tc[:, 3:4], ident[:], start=True, stop=True).then_inc(mp_tab, 1)
            pe.wait_ge(t_tab, TAB_STEPS)
            pe.wait_ge(e_loaded, 16 * N_E)

            def tile_slot(s):
                n = s.tile(1)
                if n:
                    pe.wait_ge(ma_ht, n.v + 1)
                    pe.wait_ge(mv_w, n.v + 1)
                    wait(pe, ma_relu, n.v - 1)
                    for c in range(NCH):
                        ins = mm(s_ps[n.ring(2)][:, c * P:(c + 1) * P], w_now[n.ring(4)][:, X_W1 + c * P:X_W1 + (c + 1) * P],
                                 h_mt[:, n.ring(2)], start=True, stop=True)
                    ins.then_inc(mp_up, 1)
                n = s.tile(0)
                if n:
                    pe.wait_ge(rows_loaded[n.ring(4)], 16 * (n.turn(4) + 1))
                    wait(pe, ma_ht, n.v - 1)
                    pe.transpose(t_ps[n.ring(2)][:, 0:P], rows_in[:, n.ring(4), 0:P], ident[:]).then_inc(mp_t, 1)
                n = s.tile(2)
                if n:
                    pe.wait_ge(ma_relu, n.v + 1)
                    wait(pe, mv_y, n.v - 1)
                    for c in range(NCH):
                        ins = mm([m0, m1][n.ring(2)][:, 0:P], hid[:, n.ring(2), c],
                                 w_now[n.ring(4)][:, X_W2 + c * P:X_W2 + (c + 1) * P],
                                 start=(c == 0), stop=(c == NCH - 1))
                    ins.then_inc(mp_dn, 1)

            all_tiles(pe, tile_slot)


def kernel(**inputs):
    import concourse.bacc as _bacc
    from concourse.bass_utils import run_bass_kernel_spmd as _run

    def heads_last(w):
        return w.reshape(w.shape[:-1] + (8, 2, HD)).transpose(*range(w.ndim - 1), w.ndim, w.ndim + 1, w.ndim - 1).reshape(
            w.shape)

    get = {k: np.asarray(v) for k, v in inputs.items()}
    half = P // 2
    freq = np.exp(np.arange(half, dtype=np.float32) * np.float32(-np.log(10000.0) / (half - 1))).astype(np.float32)
    arrays = {
        "x": get["x"], "bias": get["fside_Bx16xSxS_0"], "mask": get["mask_Bx1xSxS_bk0"].reshape(NB, P, P),
        "ints": np.stack([get["itok_B_34_63"].astype(np.int32), get["itok_B_6_14"].astype(np.int32)]),
    }
    a0 = {k[8:]: v for k, v in get.items() if k.startswith("L0_cond_")}
    a1 = {k[8:]: v for k, v in get.items() if k.startswith("L1_cond_")}
    columns = {
        C_FREQ: np.concatenate([freq, freq]), C_PHASE: np.repeat(np.array([0.0, 0.25], np.float32), half),
        C_BADA_S: a0["b_ada"][0:P], C_BADA_H: a0["b_ada"][P:], C_BQ: heads_last(a0["bq"]), C_BK: heads_last(a0["bk"]),
        C_G2: a0["g2"], C_BETA2: a0["beta2"], C_LNG: a1["ln_g"], C_LNB: a1["ln_b"], C_HB1: a1["hyp_b1"],
        C_HB2: a1["hyp_b2"], C_SB1: np.concatenate([a1["sty_b1"], np.zeros(half, np.float32)]),
        C_SB2G: a1["sty_b2"][0:P], C_SB2B: a1["sty_b2"][P:]}
    arrays["cols"] = np.stack([columns[c] for c in range(N_COLS)], axis=1)
    arrays["w_sq"] = np.concatenate([a0["W_ada"], heads_last(a0["Wq"]), heads_last(a0["Wk"]), a0["Wv"], a0["Wo"],
                                     a1["hyp_w2"], a1["sty_w1"], a1["router_w"]], axis=1)
    arrays["w_64"] = np.concatenate([a1["hyp_w1"], a1["sty_w2"]], axis=1)
    arrays["rows"] = np.stack([a0["bv"], a0["bo"], a0["b2"]])
    arrays["w1"], arrays["w2"] = a0["W1"], a0["W2"]
    arrays["b1"] = a0["b1"].reshape(NCH, P)
    arrays["exp_b1"] = a1["exp_b1"].reshape(E, NCH, P).transpose(2, 0, 1)
    for name in ("subj_emb", "exp_w1", "exp_w2", "exp_b2"):
        arrays[name] = a1[name]
    nc = _bacc.Bacc("TRN2", target_bir_lowering=False, num_devices=1)
    arrays = {f"in_{k}_dram": np.ascontiguousarray(v) for k, v in arrays.items()}
    a = {k[3:-5]: nc.dram_tensor(k, v.shape, mybir.dt.from_np(v.dtype), kind="ExternalInput").ap()
         for k, v in arrays.items()}
    out = nc.dram_tensor("out_0_dram", (NB, P, P), F32, kind="ExternalOutput").ap()
    build(nc, a, out)
    r = _run(nc, [arrays], core_ids=[0])
    return r.results[0]["out_0_dram"]
```

```python
from contextlib import ExitStack

import numpy as np

import concourse.bass as bass
from concourse import mybir

ALU = mybir.AluOpType
ACT = mybir.ActivationFunctionType
AX = mybir.AxisListType
F32 = mybir.dt.float32
BF16 = mybir.dt.bfloat16
I32 = mybir.dt.int32
U32 = mybir.dt.uint32
U8 = mybir.dt.uint8

P = 128
NB = 32
H, HD = 16, 8
FF = 512
NCH = FF // P
E = 8
TOPK = 2
Q_PART = [0, 0, 0, 1, 1, 1, 2, 2]
K_PART = [0, 1, 2, 0, 1, 2, 0, 1]
BK = 64 + NCH
VC = HD + 1
VW = 8 * VC
MASKED = -3.0e38
W_WIDTH = [2 * P, P, P, P, P, P, 64, 8]
W_AT = [sum(W_WIDTH[:k]) for k in range(len(W_WIDTH))]
W_COLS = sum(W_WIDTH)
ROW = 138
DEST, GATE = 136, 137
TOKENS = NB * P
REGION = TOKENS + P
MAX_TILES = TOPK * TOKENS // P + E - 1
TILES = -(-MAX_TILES // 4) * 4
NOWHERE = 4 * TOPK * TOKENS
SUMS = [(0, 8), (8, 8), (16, 8), (24, 4), (28, 4)]
EPS, EPS_T = 1e-5, 1e-8


X_W1, X_W2, X_B1, X_B2, EXPERT = 0, FF, 2 * FF, 2 * FF + NCH, 2 * FF + NCH + P
(C_BADA_S, C_BADA_H, C_BQ, C_BK, C_G2, C_BETA2, C_LNG, C_LNB, C_HB1, C_HB2, C_SB1, C_SB2G, C_SB2B, C_FREQ,
 C_PHASE) = range(15)
N_COLS = 15


class At:

    def __init__(self, unit, i, c, count):
        self.unit, self.i, self.c, self.count = unit, i, c, count

    @property
    def v(self):
        return self.i * self.unit + self.c

    def ring(self, r):
        return self.c % r

    def turn(self, r):
        return self.i * (self.unit // r) + self.c // r

    def __bool__(self):
        return not isinstance(self.i, int) or 0 <= self.v < self.count


STEP = 4


class Slot:

    def __init__(self, i, b):
        self.i, self.b, self.odd = i, b, b % 2 == 1

    def tile(self, lag):
        return At(STEP, self.i, self.b - lag, TILES)

    def batch(self, lag):
        return At(STEP, self.i, self.b - lag, NB)

    def pair(self, ahead):
        return At(STEP // 2, self.i, (self.b + ahead) // 2, NB // 2)


def batch_at(k):
    return At(STEP, 0, k, NB)


def pair_at(k):
    return At(STEP // 2, 0, k, NB // 2)


def tile_at(k):
    return At(STEP, 0, k, TILES)


def wait(eng, sem, value):
    if not isinstance(value, int) or value > 0:
        eng.wait_ge(sem, value)


def wait_first(eng, *options):
    for exists, sem, value in options:
        if exists:
            wait(eng, sem, value)
            return


def settle(eng, n):
    if not isinstance(n.i, int):
        eng.nop(nofuse=True)


FIRST_SLOT, LAST_SLOT = -4, NB + 5


def all_slots(eng, slot, after=None):
    for s in range(FIRST_SLOT, 2 * STEP):
        slot(Slot(0, s))
        if after and s in after:
            after[s]()
    with eng.Fori(2, NB // STEP - 2) as i:
        for b in range(STEP):
            slot(Slot(i, b))
    for s in range(NB - 2 * STEP, LAST_SLOT + 1):
        slot(Slot(0, s))


def all_tiles(eng, slot):
    for s in range(2 * STEP):
        slot(Slot(0, s))
    with eng.Fori(2, TILES // STEP) as i:
        for b in range(STEP):
            slot(Slot(i, b))
    for s in range(TILES, TILES + 4):
        slot(Slot(0, s))


def build(nc, a, out):
    ctx = ExitStack()
    with ctx:
        def sb(name, shape, dt=F32):
            return ctx.enter_context(nc.sbuf_tensor(name, shape, dt))

        def sem(name):
            return ctx.enter_context(nc.semaphore(name))

        part_scr = nc.dram_tensor("part_scr", (2, 6, P, 2 * P), BF16, kind="Internal").ap()
        rows_scr = nc.dram_tensor("rows_scr", (E * REGION, ROW), F32, kind="Internal").ap()
        y_scr = nc.dram_tensor("y_scr", (TOPK * TOKENS + P, P), F32, kind="Internal").ap()

        ident_r = sb("ident_r", [P, P + E])
        ident = ident_r[:, 0:P]
        ident_b = sb("ident_b", [P, P], BF16)
        before = sb("before", [P, P], BF16)
        ones_b = sb("ones_b", [P, P], BF16)
        m_half = sb("m_half", [P, 4])
        iota_e = sb("iota_e", [P, E])
        iota_p = sb("iota_p", [P, 1])
        dest_tab = sb("dest_tab", [P, NB, TOPK])
        w_sq = sb("w_sq", [P, W_COLS])
        w_ada, w_q, w_k, w_v, w_o, hyp_w2, sty_w1, w_r = (
            w_sq[:, at:at + n] for at, n in zip(W_AT, W_WIDTH))
        w_1 = sb("w_1", [P, FF])
        w_2 = sb("w_2", [P, NCH, P])
        cols = sb("cols", [P, N_COLS])
        b1_f = sb("b1_f", [BK, P])
        b1_r = sb("b1_r", [BK, 2, P])
        b1_t = sb("b1_t", [BK, 3, P], BF16)
        b1_p = sb("b1_p", [BK, P], BF16)
        sel = sb("sel", [BK, NCH, P], BF16)
        rows_bc = sb("rows_bc", [P, 3, P])
        bv_bc, bo_bc, b2_bc = (rows_bc[:, k] for k in range(3))
        ints = sb("ints", [P, 2, NB], I32)
        subj = sb("subj", [NB, 64])
        w_64 = sb("w_64", [64, 3 * P])
        hyp_w1, sty_w2 = w_64[:, 0:P], w_64[:, P:3 * P]
        pre = sb("pre", [P, 12, NB])
        scale1 = sb("scale1", [P, NB])
        shift = sb("shift", [P, NB])
        gamma = sb("gamma", [P, NB, 2])
        beta = sb("beta", [P, NB])
        w_e = sb("w_e", [P, E, EXPERT])
        resid = sb("resid", [P, NB, P])

        zero_row = sb("zero_row", [P, ROW])
        pad_f = sb("pad_f", [P, E])
        pad_i = sb("pad_i", [P, E], I32)
        base_e = sb("base_e", [P, E])
        run = sb("run", [P, 4, 4 + E])
        past = sb("past", [P, 3, E])
        tc = sb("tc", [P, 4])
        tab = sb("tab", [1, 2, P], I32)
        rows_in = sb("rows_in", [P, 4, ROW])
        dest_i = sb("dest_i", [P, 4], I32)
        gate_m = sb("gate_m", [P, 4])
        h_mt = sb("h_mt", [P, 2, P])
        hid = sb("hid", [P, 2, NCH, P])
        y_b = sb("y_b", [P, 2, P])
        y_g = sb("y_g", [P, 4, P])
        x_in = sb("x_in", [P, 2, 2, P])
        mask_u8 = sb("mask_u8", [P, 2, 2, P], U8)
        mask_b = sb("mask_b", [P, 2, 2, P], BF16)
        x_n = sb("x_n", [P, 2, P])
        x_t = sb("x_t", [P, 2, 2 * P])
        qk_f = sb("qk_f", [P, 2 * 2 * P])
        qk_r = sb("qk_r", [P, 2 * 2 * P])
        qk_p = sb("qk_p", [P, 3, 2, 2 * P], BF16)
        q_st = sb("q_st", [P, 2, 8, 2 * P], BF16)
        k_st = sb("k_st", [P, 2, 2, 8, 2 * P], BF16)
        v_pad = sb("v_pad", [P, 4, 2, 8, VW])
        score = sb("score", [P, 4, H, P])
        top = sb("top", [P, 2, H])
        prob = sb("prob", [P, 2, 4 * P])
        ctx_u = sb("ctx_u", [VW, 2 * P])
        r_den = sb("r_den", [P, H])
        ctx_n = sb("ctx_n", [P, P])
        ctx_t = sb("ctx_t", [P, P])
        x_2b = sb("x_2b", [P, P])
        n_2 = sb("n_2", [P, P])
        h_2 = sb("h_2", [P, P])
        up_t = sb("up_t", [P, NCH, P])
        act_1 = sb("act_1", [P, NCH, P])
        z_3 = sb("z_3", [P, P])
        h_t = sb("h_t", [P, 2, P])
        h_f = sb("h_f", [P, P])
        row = sb("row", [P, 4, TOPK, ROW])
        stat_f = sb("stat_f", [P, 2, 6])
        stat_2, stat_3, stat_t = (sb(n, [P, 6]) for n in ("stat_2", "stat_3", "stat_t"))
        mv_f = sb("mv_f", [P, 2, 2, 2])
        mv_2, mv_3, mv_t = (sb(n, [P, 2, 2]) for n in ("mv_2", "mv_3", "mv_t"))
        rs_f = sb("rs_f", [P, 2, 2])
        rs_2, rs_3, rs_t = (sb(n, [P, 2]) for n in ("rs_2", "rs_3", "rs_t"))
        coef = sb("coef", [P, 3])
        top8 = sb("top8", [P, 8])
        ix8 = sb("ix8", [P, 8], U32)
        ix_f = sb("ix_f", [P, TOPK])
        gate = sb("gate", [P, 4])
        hot = sb("hot", [P, 2, TOPK, E])
        hot_b = sb("hot_b", [P, E], BF16)
        count = sb("count", [P, E])
        pos = sb("pos", [P, E])
        pick = sb("pick", [P, TOPK, E])
        slot_f = sb("slot_f", [P, TOPK])
        slot_i = sb("slot_i", [P, 4, TOPK], I32)

        def res(n):
            return resid[:, bass.ds(n.v, 1), :].rearrange("p o d -> p (o d)")

        def bank(name):
            return ctx.enter_context(nc.psum_tensor(name, [P, 512], F32))

        s_ps = [bank("s_ps0"), bank("s_ps1")]
        t_ps = [bank("t_ps0"), bank("t_ps1")]
        c_ps = bank("c_ps")
        m0, m1, m2 = bank("m0"), bank("m1"), bank("m2")

        w_loaded, c_loaded, e_loaded = sem("w_loaded"), sem("c_loaded"), sem("e_loaded")
        const_ready = sem("const_ready")
        dve_const = sem("dve_const")
        pre_dve, pre_act, pre_pe, style_dve = sem("pre_dve"), sem("pre_act"), sem("pre_pe"), sem("style_dve")
        x_loaded = [sem(f"x_loaded{r}") for r in range(2)]
        mask_loaded = [sem(f"mask_loaded{r}") for r in range(2)]
        bias_loaded = [sem(f"bias_loaded{r}") for r in range(4)]
        parts_stored = sem("parts_stored")
        stack_loaded = [sem(f"stack_loaded{r}") for r in range(2)]
        (p_xt, p_xb, p_qk, p_v, p_s, p_t, p_pv, p_den, p_ct, p_wo, p_n2, p_up, p_dn, p_zt, p_rr, p_pos) = (
            sem(n) for n in ("p_xt", "p_xb", "p_qk", "p_v", "p_s", "p_t", "p_pv", "p_den", "p_ct", "p_wo", "p_n2",
                             "p_up", "p_dn", "p_zt", "p_rr", "p_pos"))
        (a_xt, a_qk, a_exp, a_c, a_ct, a_h2, a_tanh, a_ht, a_rr, a_gate, a_hf, a_mask,
         a_part) = (
            sem(n) for n in ("a_xt", "a_qk", "a_exp", "a_c", "a_ct", "a_h2", "a_tanh", "a_ht", "a_rr", "a_gate", "a_hf",
                             "a_mask", "a_part"))
        (v_statf, v_xn, v_xb, v_v, v_part, v_s, v_ctx, v_x2, v_n2, v_gelu, v_x3, v_z, v_statt,
         v_hf, v_route, v_pos) = (
            sem(n) for n in ("v_statf", "v_xn", "v_xb", "v_v", "v_part", "v_s", "v_ctx", "v_x2", "v_n2",
                             "v_gelu", "v_x3", "v_z", "v_statt", "v_hf", "v_route", "v_pos"))
        v_gates = sem("v_gates")
        v_mv, v_posc, v_hf3, v_rt = sem("v_mv"), sem("v_posc"), sem("v_hf3"), sem("v_rt")
        (g_rf, g_r2, g_r3, g_rt, g_sub, g_b2) = (sem(n) for n in ("g_rf", "g_r2", "g_r3", "g_rt", "g_sub", "g_b2"))
        g_rows = [sem(f"g_rows{r}") for r in range(4)]

        z_rows, z_rows_sp, z_rows_act, t_tab, mp_tab = sem("z_rows"), sem("z_rows_sp"), sem("z_rows_act"), sem("t_tab"), sem("mp_tab")
        b1_ready = sem("b1_ready")
        B1_STEPS = 14
        CONSTS = 27
        PADS_POOL, PADS_SP = 2, 5
        TAB_STEPS = 15
        rows_loaded = [sem(f"rows_loaded{r}") for r in range(4)]
        (mp_t, mp_up, mp_dn, ma_ht, ma_relu, ma_y, mv_meta, mv_w, mv_y) = (
            sem(n) for n in ("mp_t", "mp_up", "mp_dn", "ma_ht", "ma_relu", "ma_y", "mv_meta", "mv_w", "mv_y"))
        y_out = [sem(f"y_out{r}") for r in range(4)]
        y_loaded = [sem(f"y_loaded{c}") for c in range(len(SUMS))]
        summed, stored = sem("summed"), sem("stored")

        N_C, N_E, N_W = 3, 2 + 2 * E, 8
        PART = P * 2 * P

        w_now = [score[:, r].rearrange("p h t -> p (h t)")[:, 0:EXPERT] for r in range(4)]

        def outputs(b0, n, k):
            return score[:, b0 // 8, 8 * k + b0 % 8:8 * k + b0 % 8 + n, :]

        block = ctx.enter_context(nc.Block())

        @block.sync
        def _(sp):
            def load(dst, src, sem_):
                sp.dma_start(dst, src).then_inc(sem_, 16)

            load(ints[:], a["ints"].rearrange("(o k) b -> o k b", o=1).broadcast_to((P, 2, NB)), c_loaded)
            load(cols[:], a["cols"], c_loaded)
            load(x_in[:, 0], a["x"][0:2].rearrange("b t d -> t b d"), x_loaded[0])
            load(w_sq[:], a["w_sq"], c_loaded)
            load(x_in[:, 1], a["x"][2:4].rearrange("b t d -> t b d"), x_loaded[1])
            load(rows_bc[:], a["rows"].rearrange("(o k) d -> o k d", o=1).broadcast_to((P, 3, P)), w_loaded)
            load(subj[:], a["subj_emb"], w_loaded)
            load(w_64[:], a["w_64"], w_loaded)
            load(w_1[:], a["w1"], w_loaded)
            load(w_2[:], a["w2"].rearrange("(c p) n -> p c n", p=P), w_loaded)
            for k in range(3):
                load(b1_f[32 * k:32 * k + NCH], a["b1"], w_loaded)

            def load_x(j):
                wait(sp, v_xn, 2 * (j.v - 1))
                settle(sp, j)
                sp.dma_start(x_in[:, j.ring(2)], a["x"][bass.ds(j.v * 2, 2)].rearrange("b t d -> t b d")).then_inc(
                    x_loaded[j.ring(2)], 16)

            def load_mask(j):
                wait(sp, a_mask, j.v - 1)
                settle(sp, j)
                sp.dma_start(mask_u8[:, j.ring(2)], a["mask"][bass.ds(j.v * 2, 2)].rearrange("b q k -> q b k")).then_inc(
                    mask_loaded[j.ring(2)], 16)

            def load_bias(n):
                wait(sp, p_t, 4 * (n.v - 3))
                settle(sp, n)
                for h0 in (0, 8):
                    sp.dma_start(score[:, n.ring(4), h0:h0 + 8],
                                 a["bias"][bass.ds(n.v, 1), h0:h0 + 8].rearrange("o h q k -> q (o h) k")).then_inc(
                        bias_loaded[n.ring(4)], 16)

            def store_parts(j):
                if not isinstance(j.v, int) or j.v >= 2:
                    sp.wait_ge(stack_loaded[j.ring(2)], 16 * 12 * (j.turn(2)))
                settle(sp, j)
                sp.wait_ge(v_part, 4 * (j.v + 1))
                settle(sp, j)
                for half in range(2):
                    sp.dma_start(part_scr[j.ring(2), 3 * half:3 * half + 3].rearrange("a p t -> p a t"),
                                 qk_p[:, :, half, :]).then_inc(parts_stored, 16)

            def load_stack(j):
                r = j.ring(2)
                sp.wait_ge(parts_stored, 32 * (j.v + 1))
                settle(sp, j)
                wait(sp, p_s, 8 * (j.v - 1))
                settle(sp, j)
                base = r * 6 * PART
                for hh in range(2):
                    for s0, n_sl in ((0, 3), (3, 3), (6, 2)):
                        rows = slice(64 * hh + HD * s0, 64 * hh + HD * (s0 + n_sl))
                        q_src = bass.AP(tensor=part_scr.tensor, offset=base + Q_PART[s0] * PART + hh * 64 * 2 * P,
                                        ap=[[0, n_sl], [8 * 2 * P, HD], [1, 8 * 2 * P]])
                        k_src = bass.AP(tensor=part_scr.tensor, offset=base + 3 * PART + hh * 64 * 2 * P,
                                        ap=[[PART, n_sl], [8 * 2 * P, HD], [1, 8 * 2 * P]])
                        sp.dma_start(q_st[rows, r].rearrange("p a t -> p (a t)"), q_src).then_inc(stack_loaded[r], 16)
                        sp.dma_start(k_st[rows, r, hh].rearrange("p a t -> p (a t)"), k_src).then_inc(stack_loaded[r], 16)

            load_mask(pair_at(0))
            load_bias(batch_at(0))
            load_bias(batch_at(1))

            def load_w1(e):
                sp.dma_start(w_e[:, e, X_W1:X_W2], a["exp_w1"][e]).then_inc(e_loaded, 16)

            def load_w2(e):
                sp.dma_start(w_e[:, e, X_W2:X_B1].rearrange("p (c n) -> p c n", c=NCH),
                             a["exp_w2"][e].rearrange("(c p) n -> p c n", p=P)).then_inc(e_loaded, 16)

            def load_expert_biases():
                sp.dma_start(w_e[:, :, X_B1:X_B2], a["exp_b1"]).then_inc(e_loaded, 16)
                sp.dma_start(w_e[:, :, X_B2:EXPERT],
                             a["exp_b2"].rearrange("(o e) n -> o e n", o=1).broadcast_to((P, E, P))).then_inc(e_loaded, 16)

            def slot(s):
                if not s.odd and s.pair(8):
                    j = s.pair(8)
                    if not isinstance(j.v, int) or j.v >= 2:
                        load_x(j)
                if not s.odd:
                    if s.pair(2):
                        load_stack(s.pair(2))
                    if s.pair(2) and not (isinstance(s.i, int) and s.pair(2).v == 0):
                        load_mask(s.pair(2))
                if s.batch(-2) and not (isinstance(s.i, int) and s.batch(-2).v < 2):
                    load_bias(s.batch(-2))
                if s.odd and s.pair(3):
                    store_parts(s.pair(3))

            after = {2: load_expert_biases}
            for first in range(0, E, 2):
                after[3 + first // 2] = lambda e=first: (load_w1(e), load_w2(e), load_w1(e + 1), load_w2(e + 1))
            all_slots(sp, slot, after)
            sp.wait_ge(t_tab, 2)
            for e in range(PADS_SP, E):
                first = sp.value_load(pad_i[0:1, e:e + 1], min_val=0, max_val=E * REGION - P)
                sp.dma_start(rows_scr[bass.ds(first, P), :], zero_row[:, :]).then_inc(z_rows_sp, 16)
            for r in range(4):
                sp.wait_ge(g_rows[r], 32 * NB // 4)
            sp.wait_ge(z_rows, 16 * PADS_POOL)
            sp.wait_ge(z_rows_sp, 16 * (E - PADS_SP))
            sp.wait_ge(z_rows_act, 16 * (PADS_SP - PADS_POOL))
            sp.wait_ge(t_tab, TAB_STEPS)

            def load_rows(n):
                wait(sp, mp_t, n.v - 3)
                settle(sp, n)
                wait(sp, mv_meta, n.v - 3)
                settle(sp, n)
                first = sp.value_load(tab[0:1, 1, bass.ds(n.v, 1)], min_val=0, max_val=E * REGION - P)
                sp.dma_start(rows_in[:, n.ring(4)], rows_scr[bass.ds(first, P), :]).then_inc(rows_loaded[n.ring(4)], 16)

            load_rows(tile_at(0))
            load_rows(tile_at(1))

            def tile_slot(s):
                if s.tile(-2):
                    load_rows(s.tile(-2))

            all_tiles(sp, tile_slot)

            for r in range(4):
                sp.wait_ge(y_out[r], 16 * TILES // 4)
            for c, (b0, n) in enumerate(SUMS):
                for k in range(TOPK):
                    r0 = k * TOKENS + b0 * P
                    sp.dma_start(outputs(b0, n, k), y_scr[r0:r0 + n * P, :].rearrange("(b t) d -> t b d", t=P)).then_inc(
                        y_loaded[c], 16)
            for c, (b0, n) in enumerate(SUMS):
                sp.wait_ge(summed, TOPK * (c + 1))
                sp.dma_start(out[b0:b0 + n].rearrange("b t d -> t b d"), resid[:, b0:b0 + n, :]).then_inc(stored, 16)
            sp.wait_ge(stored, 16 * len(SUMS))

        @block.gpsimd
        def _(pool):
            def step(ins, n):
                ins.then_inc(const_ready, 1)
                pool.wait_ge(const_ready, n)

            step(nc.gpsimd.memset(ident[:], 0.0), 1)
            step(nc.gpsimd.affine_select(out=ident[:], in_=ident[:], compare_op=ALU.not_equal, fill=1.0, base=0,
                                         pattern=[[-1, P]], channel_multiplier=1), 2)
            step(nc.gpsimd.tensor_copy(ident_b[:], ident[:]), 3)
            step(nc.gpsimd.memset(ones_b[:], 1.0), 4)
            step(nc.gpsimd.affine_select(out=before[:], in_=ones_b[:], compare_op=ALU.is_gt, fill=0.0, base=0,
                                         pattern=[[1, P]], channel_multiplier=-1), 5)
            step(nc.gpsimd.memset(m_half[:], -0.5), 6)
            step(nc.gpsimd.iota(iota_e[:], pattern=[[1, E]], base=0, channel_multiplier=0,
                                allow_small_or_imprecise_dtypes=True), 7)
            step(nc.gpsimd.iota(iota_p[:], pattern=[[0, 1]], base=0, channel_multiplier=1,
                                allow_small_or_imprecise_dtypes=True), 8)
            step(nc.gpsimd.iota(dest_tab[:], pattern=[[P, NB], [TOKENS, TOPK]], base=0, channel_multiplier=1,
                                allow_small_or_imprecise_dtypes=True), 9)
            step(nc.gpsimd.iota(count[:], pattern=[[REGION, E]], base=0, channel_multiplier=0,
                                allow_small_or_imprecise_dtypes=True), 10)

            step(nc.gpsimd.iota(base_e[:], pattern=[[-(REGION // P), E]], base=0, channel_multiplier=0,
                                allow_small_or_imprecise_dtypes=True), 11)
            step(nc.gpsimd.memset(run[:], 0.0), 12)
            step(nc.gpsimd.memset(zero_row[:], 0.0), 13)
            step(nc.gpsimd.memset(zero_row[:, DEST:DEST + 1], float(NOWHERE)), 14)

            def sub(n, half):
                pool.wait_ge(v_s, 4 * n.v + 2 * half + 2)
                h0 = 8 * half
                sl = score[:, n.ring(4), h0:h0 + 8, :]
                nc.gpsimd.tensor_tensor(sl, sl, top[:, n.ring(2), h0:h0 + 8].unsqueeze(2).broadcast_to((P, 8, P)),
                                        ALU.subtract).then_inc(g_sub, 1)

            def scatter(n):
                pool.wait_ge(v_gates, 2 * n.v + 2)
                pool.wait_ge(v_pos, 2 * n.v + 2)
                settle(pool, n)
                for k in range(TOPK):
                    nc.gpsimd.indirect_dma_start(
                        rows_scr[:, :], bass.IndirectOffsetOnAxis(ap=slot_i[:, n.ring(4), k:k + 1], axis=0),
                        row[:, n.ring(4), k, :], None).then_inc(g_rows[n.ring(4)], 16)

            def slot(s):
                if s.batch(1):
                    sub(s.batch(1), 1)
                n = s.batch(3)
                if n:
                    wait(pool, v_x3, 4 * (n.v - 1) + 1)
                    nc.gpsimd.tensor_tensor(x_2b[:], res(n), b2_bc, ALU.add).then_inc(g_b2, 1)
                n = s.batch(4)
                if n:
                    pool.wait_ge(v_x3, 4 * n.v + 4)
                    nc.gpsimd.tensor_tensor(rs_3[:, n.ring(2):n.ring(2) + 1], mv_3[:, n.ring(2), 1:2], m_half[:, 0:1],
                                            ALU.pow).then_inc(g_r3, 1)
                if s.batch(7):
                    scatter(s.batch(7))
                if s.batch(0):
                    sub(s.batch(0), 0)
                n = s.batch(2)
                if n:
                    pool.wait_ge(v_x2, 4 * n.v + 4)
                    nc.gpsimd.tensor_tensor(rs_2[:, n.ring(2):n.ring(2) + 1], mv_2[:, n.ring(2), 1:2], m_half[:, 0:1],
                                            ALU.pow).then_inc(g_r2, 1)
                n = s.batch(4)
                if n:
                    pool.wait_ge(v_statt, 3 * n.v + 3)
                    nc.gpsimd.tensor_tensor(rs_t[:, n.ring(2):n.ring(2) + 1], mv_t[:, n.ring(2), 1:2], m_half[:, 0:1],
                                            ALU.pow).then_inc(g_rt, 1)
                if not s.odd and s.pair(6):
                    j = s.pair(6)
                    pool.wait_ge(v_statf, 4 * j.v + 4)
                    nc.gpsimd.tensor_tensor(rs_f[:, j.ring(2)], mv_f[:, j.ring(2), :, 1], m_half[:, 0:2],
                                            ALU.pow).then_inc(g_rf, 1)

            j = pair_at(0)
            pool.wait_ge(v_statf, 4 * j.v + 4)
            nc.gpsimd.tensor_tensor(rs_f[:, j.ring(2)], mv_f[:, j.ring(2), :, 1], m_half[:, 0:2],
                                    ALU.pow).then_inc(g_rf, 1)
            for hh in range(2):
                for r in range(2):
                    step(nc.gpsimd.memset(k_st[64 * hh:64 * hh + 64, r, 1 - hh].rearrange("p a t -> p (a t)").bitcast(U32),
                                          0), 15 + 2 * hh + r)
            step(nc.gpsimd.memset(v_pad[:].rearrange("p r t h c -> p (r t h c)"), 0.0), 19)
            for k in range(8):
                step(nc.gpsimd.memset(bass.AP(tensor=v_pad, offset=k * 8 * VW + HD,
                                              ap=[[4 * 2 * 8 * VW, P], [VW + VC, 8], [1, 1]]), 1.0), 20 + k)

            all_slots(pool, slot)
            scatter(batch_at(NB - 1))

            pool.wait_ge(t_tab, 2)
            for e in range(PADS_POOL):
                nc.gpsimd.indirect_dma_start(rows_scr[:, :], bass.IndirectOffsetOnAxis(ap=pad_i[:, e:e + 1], axis=0),
                                             zero_row[:, :], None).then_inc(z_rows, 16)

            def tile_slot(s):
                n = s.tile(3)
                if n:
                    pool.wait_ge(ma_y, n.v + 1)
                    settle(pool, n)
                    nc.gpsimd.indirect_dma_start(
                        y_scr[:, :], bass.IndirectOffsetOnAxis(ap=dest_i[:, n.ring(4):n.ring(4) + 1], axis=0),
                        y_g[:, n.ring(4)], None, bounds_check=TOPK * TOKENS - 1,
                        oob_is_err=False).then_inc(y_out[n.ring(4)], 16)

            all_tiles(pool, tile_slot)

        @block.scalar
        def _(act):
            def once(ins):
                ins.then_inc(pre_act, 1)

            act.wait_ge(pre_dve, 9)
            once(nc.scalar.activation(pre[:, 5], pre[:, 4], ACT.Sin))
            act.wait_ge(pre_act, 1)
            once(nc.scalar.activation(pre[:, 6], pre[:, 5], ACT.Silu))
            act.wait_ge(pre_pe, 2)
            once(nc.scalar.activation(shift[:], t_ps[1][:, 0:NB], ACT.Identity, bias=cols[:, C_BADA_H:C_BADA_H + 1]))

            def style_1():
                act.wait_ge(pre_pe, 4)
                once(nc.scalar.activation(pre[:, 7], t_ps[0][:, 0:NB], ACT.Relu, bias=cols[:, C_HB1:C_HB1 + 1]))

            def style_2():
                act.wait_ge(pre_pe, 5)
                once(nc.scalar.activation(pre[:, 8], t_ps[1][:, 0:NB], ACT.Identity, bias=cols[:, C_HB2:C_HB2 + 1]))

            def style_3():
                act.wait_ge(pre_pe, 6)
                once(nc.scalar.activation(pre[0:64, 9], c_ps[0:64, 0:NB], ACT.Relu, bias=cols[0:64, C_SB1:C_SB1 + 1]))

            def style_4():
                act.wait_ge(pre_pe, 8)
                once(nc.scalar.activation(beta[:], t_ps[1][:, 0:NB], ACT.Identity, bias=cols[:, C_SB2B:C_SB2B + 1]))

            def style_5():
                act.wait_ge(style_dve, 4)
                once(nc.scalar.activation(pre[:, 10], pre[:, 1], ACT.Exp))
                act.wait_ge(pre_act, 8)
                once(nc.scalar.activation(pre[:, 11], pre[:, 10], ACT.Ln, bias=1.0))

            def exps(n, c):
                act.wait_ge(p_t, 4 * n.v + c + 1)
                wait(act, p_pv, 4 * n.v + c - 1)
                nc.scalar.activation(prob[:, c % 2], t_ps[c % 2][:, :], ACT.Exp).then_inc(a_exp, 1)

            def slot(s):
                n = s.batch(2)
                if n:
                    act.wait_ge(p_pv, 4 * n.v + 4)
                    wait(act, p_den, n.v)
                    nc.scalar.activation(ctx_u[:, :], c_ps[0:VW, 0:2 * P], ACT.Copy).then_inc(a_c, 1)
                n = s.batch(6)
                if n:
                    act.wait_ge(p_rr, n.v + 1)
                    wait(act, g_rows[n.ring(4)], 32 * n.turn(4))
                    nc.scalar.activation(row[:, n.ring(4), :, 0:P + E],
                                         m0[:, 0:P + E].unsqueeze(1).broadcast_to((P, TOPK, P + E)),
                                         ACT.Copy).then_inc(a_rr, 1)
                p = s.batch(1)
                if p:
                    exps(p, 0)
                if not s.odd and s.pair(4):
                    j = s.pair(4)
                    act.wait_ge(p_xt, j.v + 1)
                    wait(act, p_v, j.v - 1)
                    act.wait_ge(pre_act, 3)
                    act.wait_ge(pre_dve, 12)
                    for b in range(2):
                        nc.scalar.activation(x_t[:, j.ring(2), b * P:(b + 1) * P], m0[:, b * P:(b + 1) * P],
                                             ACT.Identity, bias=shift[:, bass.ds(j.v * 2 + b, 1)],
                                             scale=scale1[:, bass.ds(j.v * 2 + b, 1)]).then_inc(a_xt, 1)
                if s.odd and s.pair(3):
                    j = s.pair(3)
                    act.wait_ge(p_qk, j.v + 1)
                    act.wait_ge(pre_dve, 10)
                    wait(act, v_part, 4 * j.v)
                    nc.scalar.activation(qk_f[:, 0:2 * P], m0[:, 0:2 * P], ACT.Identity,
                                         bias=cols[:, C_BQ:C_BQ + 1], scale=float(HD) ** -0.5).then_inc(a_qk, 1)
                    nc.scalar.activation(qk_f[:, 2 * P:4 * P], m0[:, 2 * P:4 * P], ACT.Identity,
                                         bias=cols[:, C_BK:C_BK + 1]).then_inc(a_qk, 1)
                    act.wait_ge(a_qk, 2 * j.v + 2)
                    wait(act, parts_stored, 32 * j.v)
                    nc.scalar.activation(qk_p[:, 0].rearrange("p a t -> p (a t)"), qk_f[:], ACT.Copy).then_inc(a_part, 1)
                n = s.batch(3)
                if n:
                    act.wait_ge(p_n2, n.v + 1)
                    wait(act, p_up, n.v)
                    nc.scalar.activation(h_2[:], m2[:, 0:P], ACT.Identity, bias=cols[:, C_BETA2:C_BETA2 + 1],
                                         scale=cols[:, C_G2:C_G2 + 1]).then_inc(a_h2, 1)
                if p:
                    exps(p, 1)
                n = s.batch(2)
                if n:
                    act.wait_ge(p_ct, n.v + 1)
                    wait(act, p_wo, n.v)
                    nc.scalar.activation(ctx_t[:], m1[:, 0:P], ACT.Copy).then_inc(a_ct, 1)
                n = s.batch(3)
                if n:
                    act.wait_ge(p_up, n.v + 1)
                    wait(act, v_gelu, n.v)
                    nc.scalar.activation(up_t[:], m2[:, :].rearrange("p (c t) -> p c t", c=NCH), ACT.Tanh,
                                         scale=0.851).then_inc(a_tanh, 1)
                n = s.batch(5)
                if n:
                    act.wait_ge(v_hf, n.v + 1)
                    wait(act, p_rr, n.v)
                    nc.scalar.activation(h_f[:], h_t[:, n.ring(2)], ACT.Identity, bias=coef[:, 2:3],
                                         scale=coef[:, 0:1]).then_inc(a_hf, 1)
                n = s.batch(6)
                if n:
                    act.wait_ge(v_route, 3 * n.v + 2)
                    wait(act, v_gates, 2 * n.v)
                    nc.scalar.activation(gate[:, 1:2], gate[:, 0:1], ACT.Tanh, scale=0.5).then_inc(a_gate, 1)
                if p:
                    exps(p, 2)
                n = s.batch(4)
                if n:
                    act.wait_ge(p_zt, n.v + 1)
                    nc.scalar.activation(h_t[:, n.ring(2)], m0[:, 0:P], ACT.Identity, bias=cols[:, C_LNB:C_LNB + 1],
                                         scale=cols[:, C_LNG:C_LNG + 1]).then_inc(a_ht, 1)
                if s.odd and s.pair(1):
                    j = s.pair(1)
                    act.wait_ge(mask_loaded[j.ring(2)], 16 * (j.turn(2) + 1))
                    wait(act, p_s, 8 * (j.v - 1))
                    nc.scalar.activation(mask_b[:, j.ring(2)], mask_u8[:, j.ring(2)], ACT.Copy,
                                         scale=MASKED).then_inc(a_mask, 1)
                if p:
                    exps(p, 3)

            all_slots(act, slot, {-3: style_1, -2: style_2, -1: style_3, 0: style_4, 1: style_5})

            act.wait_ge(t_tab, 2)
            for e in range(PADS_POOL, PADS_SP):
                first = act.value_load(pad_i[0:1, e:e + 1], min_val=0, max_val=E * REGION - P)
                act.dma_start(rows_scr[bass.ds(first, P), :], zero_row[:, :]).then_inc(z_rows_act, 16)
            act.wait_ge(t_tab, TAB_STEPS)

            def tile_slot(s):
                n = s.tile(0)
                if n:
                    act.wait_ge(mp_t, n.v + 1)
                    wait(act, mp_up, n.v - 1)
                    nc.scalar.activation(h_mt[:, n.ring(2)], t_ps[n.ring(2)][:, 0:P], ACT.Copy).then_inc(ma_ht, 1)
                n = s.tile(1)
                if n:
                    act.wait_ge(mp_up, n.v + 1)
                    wait(act, mp_dn, n.v - 1)
                    for c in range(NCH):
                        ins = nc.scalar.activation(hid[:, n.ring(2), c], s_ps[n.ring(2)][:, c * P:(c + 1) * P], ACT.Relu,
                                                   bias=w_now[n.ring(4)][:, X_B1 + c:X_B1 + c + 1])
                    ins.then_inc(ma_relu, 1)
                n = s.tile(2)
                if n:
                    act.wait_ge(mv_y, n.v + 1)
                    wait(act, y_out[n.ring(4)], 16 * n.turn(4))
                    nc.scalar.activation(y_g[:, n.ring(4)], y_b[:, n.ring(2)], ACT.Copy,
                                         scale=gate_m[:, n.ring(4):n.ring(4) + 1]).then_inc(ma_y, 1)

            all_tiles(act, tile_slot)

        @block.vector
        def _(dve):
            seen = [0]

            def once(ins):
                ins.then_inc(pre_dve, 1)
                seen[0] += 1
                dve.wait_ge(pre_dve, seen[0])

            def stats_f(j, between=()):
                r = j.ring(2)
                dve.wait_ge(x_loaded[r], 16 * (j.turn(2) + 1))
                settle(dve, j)
                for b in range(2):
                    nc.vector.bn_stats(stat_f[:, b], x_in[:, r, b]).then_inc(v_statf, 1)
                dve.wait_ge(v_statf, 4 * j.v + 2)
                settle(dve, j)
                for b in range(2):
                    nc.vector.bn_aggr(mv_f[:, r, b], stat_f[:, b]).then_inc(v_mv, 1)
                while between:
                    between.pop(0)()
                dve.wait_ge(v_mv, 2 * j.v + 2)
                wait(dve, g_rf, j.v - 1)
                nc.vector.tensor_scalar(mv_f[:, r, :, 1], mv_f[:, r, :, 1], EPS, None, ALU.add).then_inc(v_statf, 2)

            stats_f(pair_at(0))

            dve.wait_ge(c_loaded, 16 * N_C)
            dve.wait_ge(const_ready, 10)
            once(nc.vector.tensor_copy(pre[:, 0], ints[:, 0]))
            once(nc.vector.tensor_scalar(pre[:, 0], pre[:, 0], 0.01, 4000.0, ALU.mult, ALU.mult))
            once(nc.vector.tensor_scalar(pre[:, 1], pre[:, 0], cols[:, C_FREQ:C_FREQ + 1], None, ALU.mult))
            two_pi = 2 * np.pi
            c1 = 6.28125
            c2 = float(np.float32(np.floor((two_pi - c1) * 2 ** 20) / 2 ** 20))
            c3 = float(np.float32(two_pi - c1 - c2))
            magic = 1.5 * 2 ** 23
            once(nc.vector.tensor_scalar(pre[:, 2], pre[:, 1], 1.0 / two_pi, cols[:, C_PHASE:C_PHASE + 1],
                                         ALU.mult, ALU.add))
            once(nc.vector.tensor_scalar(pre[:, 2], pre[:, 2], magic, magic, ALU.add, ALU.subtract))
            once(nc.vector.scalar_tensor_tensor(pre[:, 3], pre[:, 2], -c1, pre[:, 1], ALU.mult, ALU.add))
            once(nc.vector.scalar_tensor_tensor(pre[:, 4], pre[:, 2], -c2, pre[:, 3], ALU.mult, ALU.add))
            once(nc.vector.scalar_tensor_tensor(pre[:, 3], pre[:, 2], -c3, pre[:, 4], ALU.mult, ALU.add))
            dve.wait_ge(pre_dve, 8)
            nc.vector.tensor_scalar(pre[:, 2], cols[:, C_PHASE:C_PHASE + 1].broadcast_to((P, NB)), two_pi, None,
                                    ALU.mult).then_inc(dve_const, 1)
            dve.wait_ge(dve_const, 1)
            nc.vector.tensor_tensor(pre[:, 4], pre[:, 3], pre[:, 2], ALU.add).then_inc(dve_const, 1)
            dve.wait_ge(dve_const, 2)
            once(nc.vector.tensor_scalar(pre[:, 4], pre[:, 4], float(np.float32(3.1415925)),
                                         -float(np.float32(3.1415925)), ALU.min, ALU.max))
            once(nc.vector.tensor_scalar(cols[:, C_BQ:C_BQ + 1], cols[:, C_BQ:C_BQ + 1], float(HD) ** -0.5, None,
                                         ALU.mult))
            once(nc.vector.tensor_scalar(pre[0:NB, 2], ints[0:NB, 1], iota_p[0:NB, 0:1], None, ALU.is_equal))

            def norm_f(j):
                r = j.ring(2)
                dve.wait_ge(g_rf, j.v + 1)
                wait(dve, p_xt, j.v)
                for b in range(2):
                    nc.vector.tensor_scalar(x_n[:, b], x_in[:, r, b], mv_f[:, r, b, 0:1], rs_f[:, r, b:b + 1],
                                            ALU.subtract, ALU.mult).then_inc(v_xn, 1)

            norm_f(pair_at(0))
            dve.wait_ge(pre_pe, 1)
            once(nc.vector.tensor_scalar(scale1[:], t_ps[0][:, 0:NB], cols[:, C_BADA_S:C_BADA_S + 1], 1.0,
                                         ALU.add, ALU.add))

            styled = [0]

            def style(ins):
                styled[0] += 1
                ins.then_inc(style_dve, 1)
                dve.wait_ge(style_dve, styled[0])

            def style_0():
                dve.wait_ge(pre_pe, 3)
                style(nc.vector.tensor_copy(pre[0:64, 3], c_ps[0:64, 0:NB]))

            def style_4():
                dve.wait_ge(pre_pe, 7)
                style(nc.vector.tensor_scalar(gamma[:, :, 0], t_ps[0][:, 0:NB], cols[:, C_SB2G:C_SB2G + 1], None,
                                              ALU.add))
                style(nc.vector.tensor_scalar(pre[:, 0], gamma[:, :, 0], -1.0, None, ALU.mult))
                style(nc.vector.tensor_tensor(pre[:, 1], pre[:, 0], gamma[:, :, 0], ALU.min))

            def style_5():
                dve.wait_ge(pre_act, 9)
                style(nc.vector.scalar_tensor_tensor(gamma[:, :, 0], gamma[:, :, 0], 0.0, pre[:, 11],
                                                     ALU.max, ALU.add))
                style(nc.vector.tensor_scalar(gamma[:, :, 0], gamma[:, :, 0], EPS_T, None, ALU.add))
                style(nc.vector.tensor_scalar(gamma[:, :, 1], gamma[:, :, 0], -1.0, None, ALU.mult))

            def scores(n, c, *between):
                between = list(between) + [None] * (4 - len(between))
                if n:
                    if c == 0:
                        dve.wait_ge(bias_loaded[n.ring(4)], 32 * (n.turn(4) + 1))
                        wait(dve, g_sub, 2 * (n.v - 1))
                    dve.wait_ge(p_s, 4 * n.v + c + 1)
                    settle(dve, n)
                for k, step in enumerate(between):
                    if n:
                        h = 4 * c + k
                        ins = nc.vector.tensor_tensor_reduce(
                            score[:, n.ring(4), h, :], s_ps[c % 2][:, k * P:(k + 1) * P], score[:, n.ring(4), h, :],
                            1.0, -3.4e38, ALU.add, ALU.max, top[:, n.ring(2), h:h + 1])
                        if k == 3:
                            ins.then_inc(v_s, 1)
                    if step:
                        step()

            def stats(n, src, st, mv, eps, s_, k):
                if not n:
                    return ()

                def first():
                    if k == 4:
                        dve.wait_ge(s_, k * n.v + 1)
                        settle(dve, n)
                    nc.vector.bn_stats(st[:], src).then_inc(s_, 1)

                def second():
                    dve.wait_ge(s_, k * n.v + k - 2)
                    settle(dve, n)
                    nc.vector.bn_aggr(mv[:, n.ring(2)], st[:]).then_inc(s_, 1)

                def third():
                    dve.wait_ge(s_, k * n.v + k - 1)
                    nc.vector.tensor_scalar(mv[:, n.ring(2), 1:2], mv[:, n.ring(2), 1:2], eps, None,
                                            ALU.add).then_inc(s_, 1)

                return first, second, third

            made = [0]

            def make(ins):
                made[0] += 1
                ins.then_inc(b1_ready, 1)
                dve.wait_ge(b1_ready, made[0])

            def b1_part(k):
                rows = slice(32 * k, 32 * k + NCH)
                if k == 0:
                    make(nc.vector.memset(b1_p[:], 0.0))
                    make(nc.vector.memset(sel[:], 0.0))
                src = b1_f[rows]
                for m in range(k):
                    make(nc.vector.tensor_copy(b1_t[rows, m], src))
                    make(nc.vector.tensor_tensor(b1_r[rows, m], src, b1_t[rows, m], ALU.subtract))
                    src = b1_r[rows, m]
                make(nc.vector.tensor_copy(b1_p[rows], src))
                make(nc.vector.tensor_copy(sel[rows], ident_b[rows, rows].unsqueeze(2).broadcast_to((NCH, NCH, P))))

            def both(one, other):
                def pair(k):
                    def step():
                        for chain in (one, other):
                            if k < len(chain):
                                chain[k]()
                    return step

                return [pair(k) for k in range(max(len(one), len(other)))]

            def places(n):
                def pick_rows():
                    nc.vector.tensor_tensor(pick[:], hot[:, n.ring(2)], pos[:].unsqueeze(1).broadcast_to((P, TOPK, E)),
                                            ALU.mult).then_inc(v_posc, 1)

                def put_dest():
                    wait(dve, g_rows[n.ring(4)], 32 * n.turn(4))
                    nc.vector.tensor_copy(row[:, n.ring(4), :, DEST],
                                          dest_tab[:, bass.ds(n.v, 1), :]).then_inc(v_posc, 2)

                def sum_rows():
                    dve.wait_ge(v_posc, 5 * n.v + 4)
                    nc.vector.tensor_reduce(slot_f[:], pick[:], AX.X, ALU.add).then_inc(v_posc, 1)

                def put_rows():
                    dve.wait_ge(v_posc, 5 * n.v + 5)
                    nc.vector.tensor_copy(slot_i[:, n.ring(4)], slot_f[:]).then_inc(v_pos, 1)

                return pick_rows, put_dest, sum_rows, put_rows

            def gates(n):
                dve.wait_ge(a_gate, n.v + 1)
                for k in range(TOPK):
                    nc.vector.tensor_scalar(row[:, n.ring(4), k, GATE:GATE + 1], gate[:, 1:2], k - 0.5, 0.5,
                                            ALU.mult, ALU.add).then_inc(v_gates, 1)

            def slot(s):
                n = s.batch(3)
                if n:
                    dve.wait_ge(g_r2, n.v + 1)
                    wait(dve, p_n2, n.v)
                    nc.vector.tensor_scalar(n_2[:], res(n), mv_2[:, n.ring(2), 0:1],
                                            rs_2[:, n.ring(2):n.ring(2) + 1], ALU.subtract, ALU.mult).then_inc(v_n2, 1)
                n = s.batch(4)
                if n:
                    dve.wait_ge(p_dn, n.v + 1)
                    dve.wait_ge(g_b2, n.v + 1)
                    wait(dve, v_z, n.v)
                    nc.vector.scalar_tensor_tensor(res(n), m2[:, 0:P], 0.5,
                                                   x_2b[:], ALU.mult, ALU.add).then_inc(v_x3, 1)
                n = s.batch(4)
                chain = stats(n, res(n), stat_3, mv_3, EPS, v_x3, 4) if n else ()
                scores(s.batch(0), 0, *both(chain, places(s.batch(7)) if s.batch(7) else ()))
                if s.batch(7):
                    gates(s.batch(7))
                n = s.batch(2)
                if n:
                    dve.wait_ge(p_den, n.v + 1)
                    c9 = m1[:, 0:2 * VW].rearrange("p (h c) -> p h c", c=VC)
                    nc.vector.reciprocal(r_den[:], c9[:, :, HD]).then_inc(v_ctx, 1)
                    dve.wait_ge(v_ctx, 2 * n.v + 1)
                    wait(dve, p_ct, n.v)
                    nc.vector.tensor_tensor(ctx_n[:].rearrange("p (h d) -> p h d", d=HD), c9[:, :, 0:HD],
                                            r_den[:].unsqueeze(2).broadcast_to((P, H, HD)), ALU.mult).then_inc(v_ctx, 1)
                n = s.batch(6)
                if n:
                    lg = row[:, n.ring(4), 0, P:P + E]
                    dve.wait_ge(a_rr, n.v + 1)
                    settle(dve, n)
                    nc.vector.max(top8[:], lg).then_inc(v_rt, 1)

                    def find(n=n, lg=lg):
                        dve.wait_ge(v_rt, 4 * n.v + 1)
                        settle(dve, n)
                        nc.vector.max_index(ix8[:], top8[:], lg).then_inc(v_rt, 1)
                        wait(dve, a_gate, n.v)
                        nc.vector.tensor_tensor(gate[:, 0:1], top8[:, 1:2], top8[:, 0:1],
                                                ALU.subtract).then_inc(v_route, 2)

                    def to_float(n=n):
                        dve.wait_ge(v_rt, 4 * n.v + 2)
                        nc.vector.tensor_copy(ix_f[:], ix8[:, 0:TOPK]).then_inc(v_rt, 1)

                    def one_hot(n=n):
                        dve.wait_ge(v_rt, 4 * n.v + 3)
                        nc.vector.tensor_tensor(hot[:, n.ring(2)], ix_f[:].unsqueeze(2).broadcast_to((P, TOPK, E)),
                                                iota_e[:].unsqueeze(1).broadcast_to((P, TOPK, E)),
                                                ALU.is_equal).then_inc(v_rt, 1)

                    def both_hot(n=n):
                        dve.wait_ge(v_rt, 4 * n.v + 4)
                        wait(dve, p_pos, n.v)
                        nc.vector.tensor_tensor(hot_b[:], hot[:, n.ring(2), 0], hot[:, n.ring(2), 1],
                                                ALU.add).then_inc(v_route, 1)

                    scores(s.batch(0), 1, find, to_float, one_hot, both_hot)
                else:
                    scores(s.batch(0), 1)
                if not s.odd and s.pair(4):
                    j = s.pair(4)
                    dve.wait_ge(p_xb, j.v + 1)
                    nc.vector.tensor_tensor(resid[:, bass.ds(j.v * 2, 2), :],
                                            m0[:, 0:2 * P].rearrange("p (b d) -> p b d", b=2),
                                            bo_bc.unsqueeze(1).broadcast_to((P, 2, P)), ALU.add).then_inc(v_xb, 1)
                if s.odd and s.pair(1):
                    j = s.pair(1)
                    dve.wait_ge(p_v, j.v + 1)
                    if isinstance(j.v, int) and j.v == 0:
                        dve.wait_ge(const_ready, CONSTS)
                    for b in range(2):
                        r = (2 * j.c + b) % 4
                        wait(dve, p_pv, 4 * (j.v * 2 + b - 3))
                        dst = bass.AP(tensor=v_pad, offset=r * 2 * 8 * VW,
                                      ap=[[4 * 2 * 8 * VW, P], [8 * VW, 2], [VW + VC, 8], [1, HD]])
                        nc.vector.tensor_tensor(dst, m0[:, b * P:(b + 1) * P].rearrange("p (t h d) -> p t h d", t=2, d=HD),
                                                bv_bc.rearrange("p (t h d) -> p t h d", t=2, d=HD),
                                                ALU.add).then_inc(v_v, 1)
                n = s.batch(5)
                if n:
                    r = n.ring(2)
                    dve.wait_ge(g_rt, n.v + 1)
                    b_n = beta[:, bass.ds(n.v, 1)]
                    wait(dve, a_hf, n.v)
                    nc.vector.tensor_tensor(coef[:, 0:2], gamma[:, bass.ds(n.v, 1), :].rearrange("p o k -> p (o k)"),
                                            rs_t[:, r:r + 1].broadcast_to((P, 2)), ALU.mult).then_inc(v_hf3, 1)
                    dve.wait_ge(v_hf3, n.v + 1)
                    nc.vector.scalar_tensor_tensor(coef[:, 2:3], mv_t[:, r, 0:1], coef[:, 1:2], b_n,
                                                   ALU.mult, ALU.add).then_inc(v_hf, 1)
                n = s.batch(4)
                if n:
                    dve.wait_ge(g_r3, n.v + 1)
                    wait(dve, p_zt, n.v)
                    nc.vector.tensor_scalar(z_3[:], res(n), mv_3[:, n.ring(2), 0:1],
                                            rs_3[:, n.ring(2):n.ring(2) + 1], ALU.subtract, ALU.mult).then_inc(v_z, 1)
                scores(s.batch(0), 2)
                n = s.batch(3)
                if n:
                    dve.wait_ge(a_tanh, n.v + 1)
                    wait(dve, p_dn, n.v)
                    nc.vector.scalar_tensor_tensor(act_1[:], up_t[:], 1.0,
                                                   m2[:, :].rearrange("p (c t) -> p c t", c=NCH),
                                                   ALU.add, ALU.mult).then_inc(v_gelu, 1)
                if s.odd and s.pair(5):
                    norm_f(s.pair(5))
                if s.odd and s.pair(3):
                    j = s.pair(3)
                    dve.wait_ge(a_part, j.v + 1)
                    flat = [qk_p[:, k].rearrange("p a t -> p (a t)") for k in range(3)]
                    nc.vector.tensor_tensor(qk_r[:], qk_f[:], flat[0], ALU.subtract).then_inc(v_part, 2)
                n = s.batch(2)
                if n:
                    dve.wait_ge(p_wo, n.v + 1)
                    nc.vector.tensor_tensor(res(n), m1[:, 0:P], res(n),
                                            ALU.add).then_inc(v_x2, 1)
                m = s.batch(6)
                if m:
                    dve.wait_ge(p_pos, m.v + 1)
                    nc.vector.tensor_tensor(pos[:], m1[:, 3 * P:3 * P + E], count[:], ALU.add).then_inc(v_posc, 1)
                scores(s.batch(0), 3, *(stats(n, res(n), stat_2, mv_2, EPS, v_x2, 4) if n else ()))
                if m:
                    dve.wait_ge(v_posc, 5 * m.v + 1)
                    nc.vector.tensor_tensor(count[:], m1[:, 3 * P + E:3 * P + 2 * E], count[:], ALU.add).then_inc(v_pos, 1)
                if s.odd and s.pair(3):
                    dve.wait_ge(v_part, 4 * j.v + 2)
                    nc.vector.tensor_copy(flat[1], qk_r[:]).then_inc(v_part, 1)
                    dve.wait_ge(v_part, 4 * j.v + 3)
                    nc.vector.tensor_tensor(flat[2], qk_r[:], flat[1], ALU.subtract).then_inc(v_part, 1)
                n = s.batch(4)
                if n:
                    dve.wait_ge(a_ht, n.v + 1)
                    settle(dve, n)
                chain = list(stats(n, h_t[:, n.ring(2)], stat_t, mv_t, EPS_T, v_statt, 3)) if n else []
                if chain:
                    chain.pop(0)()
                if not s.odd and s.pair(6):
                    stats_f(s.pair(6), chain)
                for step in chain:
                    step()

            def last_places():
                n = batch_at(NB - 1)
                for step in places(n):
                    step()
                gates(n)

            def tile_rounding():
                dve.wait_ge(const_ready, 11)
                nc.vector.tensor_scalar(base_e[:], base_e[:], 0.5 - 0.5 / P, None, ALU.add).then_inc(dve_const, 1)

            dve.wait_ge(w_loaded, 16 * N_W)
            nc.vector.tensor_copy(ident_r[:, P:P + E], w_r).then_inc(dve_const, 1)
            all_slots(dve, slot, {-4: lambda: (style_0(), tile_rounding()), -2: lambda: b1_part(0), -1: lambda: (b1_part(1), b1_part(2)),
                                  0: style_4, 1: style_5})

            last_places()

            steps = [0]

            def table(ins, n=1):
                steps[0] += n
                ins.then_inc(t_tab, n)
                dve.wait_ge(t_tab, steps[0])

            V = nc.vector
            dve.wait_ge(v_pos, 2 * NB)
            dve.wait_ge(const_ready, 12)
            table(V.tensor_scalar(pad_f[:], count[:], iota_p[:, 0:1], None, ALU.add))
            table(V.tensor_copy(pad_i[:], pad_f[:]))
            table(V.scalar_tensor_tensor(run[:, 0, 4:], count[:], 1.0 / P, base_e[:], ALU.mult, ALU.add))
            table(V.tensor_scalar(run[:, 0, 4:], run[:, 0, 4:], magic, magic, ALU.add, ALU.subtract))
            for k in range(3):
                table(V.tensor_tensor(run[:, k + 1, 4:], run[:, k, 4:], run[:, k, 4 - 2 ** k:4 + E - 2 ** k], ALU.add))
            table(V.tensor_scalar(past[:, 1], run[:, 0, 4:], -float(P), float(REGION), ALU.mult, ALU.add))
            table(V.tensor_scalar(past[:, 0, 0:E - 1], run[:, 3, 4:3 + E], iota_p[:, 0:1], None, ALU.is_le))
            table(V.tensor_reduce(tc[:, 0:1], past[:, 0, 0:E - 1], AX.X, ALU.add))
            table(V.tensor_tensor(past[:, 2, 0:E - 1], past[:, 0, 0:E - 1], past[:, 1, 0:E - 1], ALU.mult))
            table(V.tensor_reduce(tc[:, 1:2], past[:, 2, 0:E - 1], AX.X, ALU.add))
            table(V.scalar_tensor_tensor(tc[:, 2:3], iota_p[:], float(P), tc[:, 1:2], ALU.mult, ALU.add))
            table(V.tensor_tensor(tc[:, 3:4], tc[:, 2:3], count[:, E - 1:E], ALU.min))
            dve.wait_ge(mp_tab, 1)
            table(V.tensor_copy(tab[:], c_ps[0:1, 0:2 * P].rearrange("p (k t) -> p k t", k=2)))
            assert steps[0] == TAB_STEPS
            dve.wait_ge(e_loaded, 16 * N_E)

            def fetch_expert(n):
                e = dve.value_load(tab[0:1, 0, bass.ds(n.v, 1)], min_val=0, max_val=E - 1)
                wait(dve, mv_y, n.v - 3)
                nc.vector.tensor_copy(w_now[n.ring(4)], w_e[:, bass.ds(e, 1), :].rearrange("p o f -> p (o f)")).then_inc(
                    mv_w, 1)

            fetch_expert(tile_at(0))

            def tile_slot(s):
                if s.tile(-1):
                    fetch_expert(s.tile(-1))
                n = s.tile(2)
                if n:
                    dve.wait_ge(mp_dn, n.v + 1)
                    wait(dve, ma_y, n.v - 1)
                    nc.vector.tensor_tensor(y_b[:, n.ring(2)], [m0, m1][n.ring(2)][:, 0:P],
                                            w_now[n.ring(4)][:, X_B2:EXPERT], ALU.add).then_inc(mv_y, 1)
                n = s.tile(0)
                if n:
                    r = n.ring(4)
                    dve.wait_ge(rows_loaded[r], 16 * (n.turn(4) + 1))
                    wait(dve, y_out[r], 16 * n.turn(4))
                    nc.vector.tensor_copy(dest_i[:, r:r + 1], rows_in[:, r, DEST:DEST + 1])
                    nc.vector.tensor_copy(gate_m[:, r:r + 1], rows_in[:, r, GATE:GATE + 1]).then_inc(mv_meta, 1)

            all_tiles(dve, tile_slot)

            for c, (b0, n) in enumerate(SUMS):
                dve.wait_ge(y_loaded[c], 16 * TOPK)
                for k in range(TOPK):
                    nc.vector.tensor_tensor(resid[:, b0:b0 + n, :], resid[:, b0:b0 + n, :], outputs(b0, n, k),
                                            ALU.add).then_inc(summed, 1)
                    dve.wait_ge(summed, TOPK * c + k + 1)

        @block.tensor
        def _(pe):
            mm = nc.tensor.matmul

            pe.wait_ge(c_loaded, 16 * N_C)
            pe.wait_ge(pre_act, 2)
            mm(t_ps[0][:, 0:NB], w_ada[:, 0:P], pre[:, 6], start=True, stop=True).then_inc(pre_pe, 1)
            mm(t_ps[1][:, 0:NB], w_ada[:, P:2 * P], pre[:, 6], start=True, stop=True).then_inc(pre_pe, 1)
            def style_0():
                pe.wait_ge(w_loaded, 16 * N_W)
                pe.wait_ge(pre_dve, 11)
                mm(c_ps[0:64, 0:NB], subj[:], pre[0:NB, 2], start=True, stop=True).then_inc(pre_pe, 1)

            def style_1():
                pe.wait_ge(style_dve, 1)
                mm(t_ps[0][:, 0:NB], hyp_w1, pre[0:64, 3], start=True, stop=True).then_inc(pre_pe, 1)

            def style_2():
                pe.wait_ge(pre_act, 4)
                mm(t_ps[1][:, 0:NB], hyp_w2, pre[:, 7], start=True, stop=True).then_inc(pre_pe, 1)

            def style_3():
                pe.wait_ge(pre_act, 5)
                mm(c_ps[0:64, 0:NB], sty_w1, pre[:, 8], start=True, stop=True).then_inc(pre_pe, 1)
                pe.wait_ge(const_ready, 18)

            def style_4():
                pe.wait_ge(pre_act, 6)
                mm(t_ps[0][:, 0:NB], sty_w2[:, 0:P], pre[0:64, 9], start=True, stop=True).then_inc(pre_pe, 1)
                mm(t_ps[1][:, 0:NB], sty_w2[:, P:2 * P], pre[0:64, 9], start=True, stop=True).then_inc(pre_pe, 1)
                pe.wait_ge(style_dve, 2)
                pe.wait_ge(pre_act, 7)
                pe.wait_ge(const_ready, CONSTS)

            def scores(n, c):
                j_r, b = (n.c // 2) % 2, n.c % 2
                if c == 0:
                    pe.wait_ge(stack_loaded[j_r], 16 * 12 * (n.turn(4) + 1))
                    pe.wait_ge(a_mask, n.turn(2) + 1)
                wait(pe, v_s, 4 * n.v + c - 1)
                ps = s_ps[c % 2]
                mm(ps[:, :], ident_b[:], mask_b[:, j_r, b].unsqueeze(1).broadcast_to((P, 4, P)), start=True, stop=False,
                   skip_group_check=True)
                for k in range(2):
                    pr = 2 * c + k
                    ins = mm(ps[:, k * 2 * P:(k + 1) * 2 * P], q_st[:, j_r, pr, b * P:(b + 1) * P],
                             k_st[:, j_r, :, pr, b * P:(b + 1) * P], start=False, stop=True,
                             skip_group_check=True)
                ins.then_inc(p_s, 1)

            def turn(n, c):
                if c % 2 == 0:
                    pe.wait_ge(g_sub, 2 * n.v + c // 2 + 1)
                wait(pe, a_exp, 4 * n.v + c - 1)
                for k in range(4):
                    ins = pe.transpose(t_ps[c % 2][:, k * P:(k + 1) * P], score[:, n.ring(4), 4 * c + k, :], ident[:])
                ins.then_inc(p_t, 1)

            def values(n, c):
                if c == 0:
                    wait(pe, a_c, n.v)
                    pe.wait_ge(v_v, n.v + 1)
                pe.wait_ge(a_exp, 4 * n.v + c + 1)
                for k in range(4):
                    h = 4 * c + k
                    ins = mm(c_ps[0:VW, (h // 8) * P:(h // 8 + 1) * P], v_pad[:, n.ring(4), h // 8, h % 8, :],
                             prob[:, c % 2, k * P:(k + 1) * P], start=(h % 8 == 0), stop=(h % 8 == 7))
                ins.then_inc(p_pv, 1)

            def slot(s):
                n, p = s.batch(0), s.batch(1)
                if p:
                    turn(p, 0)
                if n:
                    scores(n, 0)
                rr6 = (s.batch(6), a_rr, s.batch(6).v + 1)
                zt5 = (s.batch(5), a_ht, s.batch(5).v + 1)
                if not s.odd and s.pair(4):
                    j = s.pair(4)
                    pe.wait_ge(v_xn, 2 * j.v + 2)
                    wait_first(pe, rr6, zt5, (s.pair(0), v_v, 2 * s.pair(0).v + 2), (s.pair(3), a_qk, 2 * s.pair(2).v + 2))
                    for b in range(2):
                        ins = pe.transpose(m0[:, b * P:(b + 1) * P], x_n[:, b], ident[:])
                    ins.then_inc(p_xt, 1)
                if s.odd and s.pair(3):
                    j = s.pair(3)
                    pe.wait_ge(a_xt, 2 * j.v + 2)
                    wait_first(pe, rr6, zt5, (True, v_xb, s.pair(3).v + 1))
                    mm(m0[:, 0:2 * P], w_q, x_t[:, j.ring(2)], start=True, stop=True)
                    mm(m0[:, 2 * P:4 * P], w_k, x_t[:, j.ring(2)], start=True, stop=True).then_inc(p_qk, 1)
                if s.batch(2):
                    d = s.batch(2)
                    pe.wait_ge(a_c, d.v + 1)
                    wait_first(pe, (s.batch(7), v_pos, 2 * s.batch(7).v + 1), (s.batch(3), v_x2, 4 * s.batch(3).v + 1))
                    for t in range(2):
                        ins = pe.transpose(m1[:, t * VW:(t + 1) * VW], ctx_u[:, t * P:(t + 1) * P], ident[0:VW, 0:VW])
                    ins.then_inc(p_den, 1)
                if p:
                    values(p, 0)
                if s.batch(3):
                    d = s.batch(3)
                    pe.wait_ge(v_n2, d.v + 1)
                    wait(pe, v_x3, 4 * (d.v - 1) + 1)
                    pe.transpose(m2[:, 0:P], n_2[:], ident[:]).then_inc(p_n2, 1)
                if p:
                    turn(p, 1)
                if n:
                    scores(n, 1)
                if not s.odd and s.pair(4):
                    j = s.pair(4)
                    pe.wait_ge(a_xt, 2 * j.v + 2)
                    for b in range(2):
                        ins = pe.transpose(m0[:, b * P:(b + 1) * P], x_t[:, j.ring(2), b * P:(b + 1) * P], ident[:])
                    ins.then_inc(p_xb, 1)
                if s.odd and s.pair(1):
                    j = s.pair(1)
                    wait_first(pe, (s.pair(3), a_qk, 2 * s.pair(3).v + 2), rr6, zt5)
                    for b in range(2):
                        ins = mm(m0[:, b * P:(b + 1) * P], x_t[:, j.ring(2), b * P:(b + 1) * P], w_v,
                                 start=True, stop=True)
                    ins.then_inc(p_v, 1)
                if s.batch(2):
                    d = s.batch(2)
                    pe.wait_ge(v_ctx, 2 * d.v + 2)
                    pe.transpose(m1[:, 0:P], ctx_n[:], ident[:]).then_inc(p_ct, 1)
                if s.batch(3):
                    d = s.batch(3)
                    pe.wait_ge(a_h2, d.v + 1)
                    mm(m2[:, :], b1_p[:], sel[:].rearrange("p c t -> p (c t)"), start=True, stop=False,
                       skip_group_check=True)
                    for c in range(NCH):
                        ins = mm(m2[:, c * P:(c + 1) * P], w_1[:, c * P:(c + 1) * P], h_2[:], start=False, stop=True,
                                 skip_group_check=True)
                    ins.then_inc(p_up, 1)
                if p:
                    values(p, 1)
                if p:
                    turn(p, 2)
                if n:
                    scores(n, 2)
                if s.batch(4):
                    d = s.batch(4)
                    pe.wait_ge(v_z, d.v + 1)
                    wait_first(pe, (not s.odd and s.pair(4), v_xb, s.pair(4).v + 1),
                               (s.odd and s.pair(1), v_v, 2 * s.pair(1).v + 2), rr6, zt5)
                    pe.transpose(m0[:, 0:P], z_3[:], ident[:]).then_inc(p_zt, 1)
                if s.batch(2):
                    pe.wait_ge(a_ct, s.batch(2).v + 1)
                if s.batch(6):
                    d = s.batch(6)
                    pe.wait_ge(v_route, 3 * d.v + 3)
                    mm(m1[:, 3 * P:3 * P + E], before[:], hot_b[:], start=True, stop=True)
                    ins = mm(m1[:, 3 * P + E:3 * P + 2 * E], ones_b[:], hot_b[:], start=True, stop=True)
                    ins.then_inc(p_pos, 1)
                if s.batch(2):
                    d = s.batch(2)
                    mm(m1[:, 0:P], ctx_t[:], w_o, start=True, stop=True).then_inc(p_wo, 1)
                if p:
                    values(p, 2)
                if p:
                    turn(p, 3)
                if n:
                    scores(n, 3)
                if s.batch(5):
                    d = s.batch(5)
                    pe.wait_ge(a_hf, d.v + 1)
                    wait_first(pe, (s.batch(4), a_ht, s.batch(4).v + 1), rr6)
                    mm(m0[:, 0:P + E], h_f[:], ident_r[:], start=True, stop=True).then_inc(p_rr, 1)
                if s.batch(3):
                    d = s.batch(3)
                    pe.wait_ge(v_gelu, d.v + 1)
                    for c in range(NCH):
                        ins = mm(m2[:, 0:P], act_1[:, c], w_2[:, c], start=(c == 0), stop=(c == NCH - 1))
                    ins.then_inc(p_dn, 1)
                if p:
                    values(p, 3)

            all_slots(pe, slot, {-4: style_0, -3: style_1, -2: style_2, -1: style_3, 0: style_4,
                                 2: lambda: pe.wait_ge(b1_ready, B1_STEPS)})

            pe.wait_ge(t_tab, TAB_STEPS - 1)
            mm(c_ps[0:1, 0:P], tc[:, 0:1], ident[:], start=True, stop=True)
            mm(c_ps[0:1, P:2 * P], tc[:, 3:4], ident[:], start=True, stop=True).then_inc(mp_tab, 1)
            pe.wait_ge(t_tab, TAB_STEPS)
            pe.wait_ge(e_loaded, 16 * N_E)

            def tile_slot(s):
                n = s.tile(1)
                if n:
                    pe.wait_ge(ma_ht, n.v + 1)
                    pe.wait_ge(mv_w, n.v + 1)
                    wait(pe, ma_relu, n.v - 1)
                    for c in range(NCH):
                        ins = mm(s_ps[n.ring(2)][:, c * P:(c + 1) * P], w_now[n.ring(4)][:, X_W1 + c * P:X_W1 + (c + 1) * P],
                                 h_mt[:, n.ring(2)], start=True, stop=True)
                    ins.then_inc(mp_up, 1)
                n = s.tile(0)
                if n:
                    pe.wait_ge(rows_loaded[n.ring(4)], 16 * (n.turn(4) + 1))
                    wait(pe, ma_ht, n.v - 1)
                    pe.transpose(t_ps[n.ring(2)][:, 0:P], rows_in[:, n.ring(4), 0:P], ident[:]).then_inc(mp_t, 1)
                n = s.tile(2)
                if n:
                    pe.wait_ge(ma_relu, n.v + 1)
                    wait(pe, mv_y, n.v - 1)
                    for c in range(NCH):
                        ins = mm([m0, m1][n.ring(2)][:, 0:P], hid[:, n.ring(2), c],
                                 w_now[n.ring(4)][:, X_W2 + c * P:X_W2 + (c + 1) * P],
                                 start=(c == 0), stop=(c == NCH - 1))
                    ins.then_inc(mp_dn, 1)

            all_tiles(pe, tile_slot)


def kernel(**inputs):
    import concourse.bacc as _bacc
    from concourse.bass_utils import run_bass_kernel_spmd as _run

    def heads_last(w):
        return w.reshape(w.shape[:-1] + (8, 2, HD)).transpose(*range(w.ndim - 1), w.ndim, w.ndim + 1, w.ndim - 1).reshape(
            w.shape)

    get = {k: np.asarray(v) for k, v in inputs.items()}
    half = P // 2
    freq = np.exp(np.arange(half, dtype=np.float32) * np.float32(-np.log(10000.0) / (half - 1))).astype(np.float32)
    arrays = {
        "x": get["x"], "bias": get["fside_Bx16xSxS_0"], "mask": get["mask_Bx1xSxS_bk0"].reshape(NB, P, P),
        "ints": np.stack([get["itok_B_34_63"].astype(np.int32), get["itok_B_6_14"].astype(np.int32)]),
    }
    a0 = {k[8:]: v for k, v in get.items() if k.startswith("L0_cond_")}
    a1 = {k[8:]: v for k, v in get.items() if k.startswith("L1_cond_")}
    columns = {
        C_FREQ: np.concatenate([freq, freq]), C_PHASE: np.repeat(np.array([0.0, 0.25], np.float32), half),
        C_BADA_S: a0["b_ada"][0:P], C_BADA_H: a0["b_ada"][P:], C_BQ: heads_last(a0["bq"]), C_BK: heads_last(a0["bk"]),
        C_G2: a0["g2"], C_BETA2: a0["beta2"], C_LNG: a1["ln_g"], C_LNB: a1["ln_b"], C_HB1: a1["hyp_b1"],
        C_HB2: a1["hyp_b2"], C_SB1: np.concatenate([a1["sty_b1"], np.zeros(half, np.float32)]),
        C_SB2G: a1["sty_b2"][0:P], C_SB2B: a1["sty_b2"][P:]}
    arrays["cols"] = np.stack([columns[c] for c in range(N_COLS)], axis=1)
    arrays["w_sq"] = np.concatenate([a0["W_ada"], heads_last(a0["Wq"]), heads_last(a0["Wk"]), a0["Wv"], a0["Wo"],
                                     a1["hyp_w2"], a1["sty_w1"], a1["router_w"]], axis=1)
    arrays["w_64"] = np.concatenate([a1["hyp_w1"], a1["sty_w2"]], axis=1)
    arrays["rows"] = np.stack([a0["bv"], a0["bo"], a0["b2"]])
    arrays["w1"], arrays["w2"] = a0["W1"], a0["W2"]
    arrays["b1"] = a0["b1"].reshape(NCH, P)
    arrays["exp_b1"] = a1["exp_b1"].reshape(E, NCH, P).transpose(2, 0, 1)
    for name in ("subj_emb", "exp_w1", "exp_w2", "exp_b2"):
        arrays[name] = a1[name]
    nc = _bacc.Bacc("TRN2", target_bir_lowering=False, num_devices=1)
    arrays = {f"in_{k}_dram": np.ascontiguousarray(v) for k, v in arrays.items()}
    a = {k[3:-5]: nc.dram_tensor(k, v.shape, mybir.dt.from_np(v.dtype), kind="ExternalInput").ap()
         for k, v in arrays.items()}
    out = nc.dram_tensor("out_0_dram", (NB, P, P), F32, kind="ExternalOutput").ap()
    build(nc, a, out)
    r = _run(nc, [arrays], core_ids=[0])
    return r.results[0]["out_0_dram"]
```
